# Optimizing a Trainium2 kernel written in Bass

```python
import numpy as np
import jax
import jax.numpy as jnp

def _softmax(x, axis=-1):
    return jax.nn.softmax(x, axis=axis)

def _gelu(x):
    return jax.nn.gelu(x, approximate=True)

def _silu(x):
    return jax.nn.silu(x)

def _sigmoid(x):
    return jax.nn.sigmoid(x)

def _layernorm(x, axis=-1, eps=1e-05):
    m = jnp.mean(x, axis=axis, keepdims=True)
    v = jnp.var(x, axis=axis, keepdims=True)
    return (x - m) / jnp.sqrt(v + eps)

def _scatter_add(tgt, idx, src, axis=0):
    return tgt.at[idx].add(src)

def _segment_sum(src, seg, n):
    return jax.ops.segment_sum(src, seg, n)
kernel_name = 'mk_adaln_d1_jaxref_r8_120152'

def setup_inputs(seed: int=0):
    np.random.seed(seed)
    _w = jnp.asarray

    def _L0_attn_setup():
        import jax, jax.numpy as jnp
        import numpy as np
        BASE_THETA = 0.5
        K_DOP = 0.2
        K_NOR = 0.15
        K_SERO = 0.1
        DIM = 128
        key = jax.random.key(seed)
        ks = jax.random.split(key, 9)
        scale = 1.0 / np.sqrt(DIM)
        x = jax.random.normal(ks[0], (2, 256, DIM), dtype=jnp.float32)
        Wq = jax.random.normal(ks[1], (DIM, DIM), dtype=jnp.float32) * scale
        bq = jnp.zeros((DIM,), dtype=jnp.float32)
        Wk = jax.random.normal(ks[2], (DIM, DIM), dtype=jnp.float32) * scale
        bk = jnp.zeros((DIM,), dtype=jnp.float32)
        Wv = jax.random.normal(ks[3], (DIM, DIM), dtype=jnp.float32) * scale
        bv = jnp.zeros((DIM,), dtype=jnp.float32)
        Wo = jax.random.normal(ks[4], (DIM, DIM), dtype=jnp.float32) * scale
        bo = jnp.zeros((DIM,), dtype=jnp.float32)
        return {'x': x, 'Wq': Wq, 'bq': bq, 'Wk': Wk, 'bk': bk, 'Wv': Wv, 'bv': bv, 'Wo': Wo, 'bo': bo}
    _L0_attn_in = _L0_attn_setup()

    def _L0_ffn_setup():
        import jax, jax.numpy as jnp
        import numpy as np
        DIM = 128
        DEPTH = 6
        HEADS = 16
        DIM_HEAD = 64
        WINDOW = 32
        INNER = HEADS * DIM_HEAD
        DIM_INNER = int(DIM * 4 * 2 / 3)
        QK_SCALE = 8.0

        def shift_tokens(t):
            a, s = jnp.split(t, 2, -1)
            s = jnp.pad(s, ((0, 0), (1, 0), (0, 0)))[:, :-1]
            return jnp.concatenate([a, s], -1)

        def l2norm(t):
            return t / jnp.maximum(jnp.linalg.norm(t, axis=-1, keepdims=True), 1e-12)

        def rotate_half(x):
            x1, x2 = jnp.split(x, 2, -1)
            return jnp.concatenate([-x2, x1], -1)

        def rotary_tables(n):
            half = jnp.arange(0, DIM_HEAD, 2, dtype=jnp.float32)
            inv_freq = 1.0 / 10000.0 ** (half / DIM_HEAD)
            t = jnp.arange(n, dtype=jnp.float32)
            freqs = t[:, None] * inv_freq[None, :]
            freqs = jnp.concatenate([freqs, freqs], -1)
            base_scale = (half + 0.4 * DIM_HEAD) / (1.4 * DIM_HEAD)
            power = (t - n // 2) / (WINDOW // 2)
            scale = base_scale[None, :] ** power[:, None]
            scale = jnp.concatenate([scale, scale], -1)
            return (freqs, scale)

        def local_attention(q, k, v):
            b, h, n, d = q.shape
            w = WINDOW
            nw = n // w
            bq = q.reshape(b, h, nw, w, d)
            bk = k.reshape(b, h, nw, w, d)
            bv = v.reshape(b, h, nw, w, d)

            def look(t):
                p = jnp.pad(t, ((0, 0), (0, 0), (1, 0), (0, 0), (0, 0)))
                return jnp.concatenate([p[:, :, :nw], p[:, :, 1:]], axis=3)
            bk2, bv2 = (look(bk), look(bv))
            seq = jnp.arange(n).reshape(nw, w)
            seq_p = jnp.pad(seq, ((1, 0), (0, 0)), constant_values=-1)
            jt = jnp.concatenate([seq_p[:nw], seq_p[1:]], axis=1)
            it = seq[:, :, None]
            jb = jt[:, None, :]
            mask = (it < jb) | (it > jb + w) | (jb == -1)
            sim = jnp.einsum('bhwie,bhwje->bhwij', bq, bk2) * QK_SCALE
            sim = jnp.where(mask, -jnp.finfo(sim.dtype).max, sim)
            attn = jax.nn.softmax(sim, -1)
            out = jnp.einsum('bhwij,bhwje->bhwie', attn, bv2)
            return out.reshape(b, h, n, d)

        def attn_layer(x, Wqkv, qs, ksc, Wo):
            b, n, _ = x.shape
            qkv = x @ Wqkv
            q, k, v = jnp.split(qkv, 3, -1)
            sh = lambda t: t.reshape(b, n, HEADS, DIM_HEAD).transpose(0, 2, 1, 3)
            q, k, v = (sh(q), sh(k), sh(v))
            q = l2norm(q) * qs
            k = l2norm(k) * ksc
            freqs, scale = rotary_tables(n)
            cos, sin = (jnp.cos(freqs), jnp.sin(freqs))
            q = q * cos * scale + rotate_half(q) * sin * scale
            inv = 1.0 / scale
            k = k * cos * inv + rotate_half(k) * sin * inv
            out = local_attention(q, k, v)
            out = out.transpose(0, 2, 1, 3).reshape(b, n, INNER)
            return out @ Wo

        def ffn_layer(x, g, bln, W1, b1, W2, b2):
            mu = x.mean(-1, keepdims=True)
            var = ((x - mu) ** 2).mean(-1, keepdims=True)
            xn = (x - mu) / jnp.sqrt(var + 1e-05) * g + bln
            hg = xn @ W1 + b1
            a, gate = jnp.split(hg, 2, -1)
            return a * jax.nn.gelu(gate, approximate=False) @ W2 + b2
        key = jax.random.key(seed)
        ks = jax.random.split(key, 8)
        B, N = (2, 256)
        init = lambda k, shape: jax.random.normal(k, shape, jnp.float32) * 0.02
        return {'x': jax.random.normal(ks[0], (B, N, DIM), jnp.float32), 'Wqkv': init(ks[1], (DEPTH, DIM, 3 * INNER)), 'q_scale': jnp.ones((DEPTH, DIM_HEAD), jnp.float32), 'k_scale': jnp.ones((DEPTH, DIM_HEAD), jnp.float32), 'Wo': init(ks[2], (DEPTH, INNER, DIM)), 'ln_g': jnp.ones((DEPTH, DIM), jnp.float32), 'ln_b': jnp.zeros((DEPTH, DIM), jnp.float32), 'W1': init(ks[3], (DEPTH, DIM, 2 * DIM_INNER)), 'b1': jnp.zeros((DEPTH, 2 * DIM_INNER), jnp.float32), 'W2': init(ks[4], (DEPTH, DIM_INNER, DIM)), 'b2': jnp.zeros((DEPTH, DIM), jnp.float32)}
    _L0_ffn_in = _L0_ffn_setup()
    _L0_c = _w((lambda *s: np.random.randn(*s).astype(np.float32) * 0.05)(8, 128))
    _L0_wmod = _w((lambda *s: np.random.randn(*s).astype(np.float32) * 0.05)(128, 6 * 128) * 128 ** (-0.5))
    _d = {'L0_attn_x': _L0_attn_in['x'], 'L0_attn_Wq': _L0_attn_in['Wq'], 'L0_attn_bq': _L0_attn_in['bq'], 'L0_attn_Wk': _L0_attn_in['Wk'], 'L0_attn_bk': _L0_attn_in['bk'], 'L0_attn_Wv': _L0_attn_in['Wv'], 'L0_attn_bv': _L0_attn_in['bv'], 'L0_attn_Wo': _L0_attn_in['Wo'], 'L0_attn_bo': _L0_attn_in['bo'], 'L0_ffn_Wqkv': _L0_ffn_in['Wqkv'], 'L0_ffn_q_scale': _L0_ffn_in['q_scale'], 'L0_ffn_k_scale': _L0_ffn_in['k_scale'], 'L0_ffn_Wo': _L0_ffn_in['Wo'], 'L0_ffn_ln_g': _L0_ffn_in['ln_g'], 'L0_ffn_ln_b': _L0_ffn_in['ln_b'], 'L0_ffn_W1': _L0_ffn_in['W1'], 'L0_ffn_b1': _L0_ffn_in['b1'], 'L0_ffn_W2': _L0_ffn_in['W2'], 'L0_ffn_b2': _L0_ffn_in['b2'], 'L0_c': _L0_c, 'L0_wmod': _L0_wmod}
    _x0 = _d['L0_attn_x']
    _d['L0_attn_x'] = jax.random.normal(jax.random.fold_in(jax.random.key(seed), 1), (8, 512, 128), dtype=_x0.dtype)
    del _x0
    return _d

def reference(L0_attn_x, L0_attn_Wq, L0_attn_bq, L0_attn_Wk, L0_attn_bk, L0_attn_Wv, L0_attn_bv, L0_attn_Wo, L0_attn_bo, L0_ffn_Wqkv, L0_ffn_q_scale, L0_ffn_k_scale, L0_ffn_Wo, L0_ffn_ln_g, L0_ffn_ln_b, L0_ffn_W1, L0_ffn_b1, L0_ffn_W2, L0_ffn_b2, L0_c, L0_wmod):

    def _L0_attn_ref(x, Wq, bq, Wk, bk, Wv, bv, Wo, bo):
        import jax, jax.numpy as jnp
        import numpy as np
        BASE_THETA = 0.5
        K_DOP = 0.2
        K_NOR = 0.15
        K_SERO = 0.1
        DIM = 128
        q = jnp.einsum('bsd,ed->bse', x, Wq) + bq
        k = jnp.einsum('bsd,ed->bse', x, Wk) + bk
        v = jnp.einsum('bsd,ed->bse', x, Wv) + bv
        qk = jnp.einsum('bsd,btd->bst', q, k)
        theta = BASE_THETA + K_DOP * jax.nn.sigmoid(qk) + K_NOR * jnp.tanh(qk) + K_SERO * jax.nn.relu(qk)
        attn = jax.nn.softmax(theta, axis=-1)
        out = jnp.einsum('bst,btd->bsd', attn, v)
        return jnp.einsum('bsd,ed->bse', out, Wo) + bo

    def _L0_ffn_ref(x, Wqkv, q_scale, k_scale, Wo, ln_g, ln_b, W1, b1, W2, b2):
        import jax, jax.numpy as jnp
        import numpy as np
        DIM = 128
        DEPTH = 6
        HEADS = 16
        DIM_HEAD = 64
        WINDOW = 32
        INNER = HEADS * DIM_HEAD
        DIM_INNER = int(DIM * 4 * 2 / 3)
        QK_SCALE = 8.0

        def shift_tokens(t):
            a, s = jnp.split(t, 2, -1)
            s = jnp.pad(s, ((0, 0), (1, 0), (0, 0)))[:, :-1]
            return jnp.concatenate([a, s], -1)

        def l2norm(t):
            return t / jnp.maximum(jnp.linalg.norm(t, axis=-1, keepdims=True), 1e-12)

        def rotate_half(x):
            x1, x2 = jnp.split(x, 2, -1)
            return jnp.concatenate([-x2, x1], -1)

        def rotary_tables(n):
            half = jnp.arange(0, DIM_HEAD, 2, dtype=jnp.float32)
            inv_freq = 1.0 / 10000.0 ** (half / DIM_HEAD)
            t = jnp.arange(n, dtype=jnp.float32)
            freqs = t[:, None] * inv_freq[None, :]
            freqs = jnp.concatenate([freqs, freqs], -1)
            base_scale = (half + 0.4 * DIM_HEAD) / (1.4 * DIM_HEAD)
            power = (t - n // 2) / (WINDOW // 2)
            scale = base_scale[None, :] ** power[:, None]
            scale = jnp.concatenate([scale, scale], -1)
            return (freqs, scale)

        def local_attention(q, k, v):
            b, h, n, d = q.shape
            w = WINDOW
            nw = n // w
            bq = q.reshape(b, h, nw, w, d)
            bk = k.reshape(b, h, nw, w, d)
            bv = v.reshape(b, h, nw, w, d)

            def look(t):
                p = jnp.pad(t, ((0, 0), (0, 0), (1, 0), (0, 0), (0, 0)))
                return jnp.concatenate([p[:, :, :nw], p[:, :, 1:]], axis=3)
            bk2, bv2 = (look(bk), look(bv))
            seq = jnp.arange(n).reshape(nw, w)
            seq_p = jnp.pad(seq, ((1, 0), (0, 0)), constant_values=-1)
            jt = jnp.concatenate([seq_p[:nw], seq_p[1:]], axis=1)
            it = seq[:, :, None]
            jb = jt[:, None, :]
            mask = (it < jb) | (it > jb + w) | (jb == -1)
            sim = jnp.einsum('bhwie,bhwje->bhwij', bq, bk2) * QK_SCALE
            sim = jnp.where(mask, -jnp.finfo(sim.dtype).max, sim)
            attn = jax.nn.softmax(sim, -1)
            out = jnp.einsum('bhwij,bhwje->bhwie', attn, bv2)
            return out.reshape(b, h, n, d)

        def attn_layer(x, Wqkv, qs, ksc, Wo):
            b, n, _ = x.shape
            qkv = x @ Wqkv
            q, k, v = jnp.split(qkv, 3, -1)
            sh = lambda t: t.reshape(b, n, HEADS, DIM_HEAD).transpose(0, 2, 1, 3)
            q, k, v = (sh(q), sh(k), sh(v))
            q = l2norm(q) * qs
            k = l2norm(k) * ksc
            freqs, scale = rotary_tables(n)
            cos, sin = (jnp.cos(freqs), jnp.sin(freqs))
            q = q * cos * scale + rotate_half(q) * sin * scale
            inv = 1.0 / scale
            k = k * cos * inv + rotate_half(k) * sin * inv
            out = local_attention(q, k, v)
            out = out.transpose(0, 2, 1, 3).reshape(b, n, INNER)
            return out @ Wo

        def ffn_layer(x, g, bln, W1, b1, W2, b2):
            mu = x.mean(-1, keepdims=True)
            var = ((x - mu) ** 2).mean(-1, keepdims=True)
            xn = (x - mu) / jnp.sqrt(var + 1e-05) * g + bln
            hg = xn @ W1 + b1
            a, gate = jnp.split(hg, 2, -1)
            return a * jax.nn.gelu(gate, approximate=False) @ W2 + b2
        for i in range(DEPTH):
            x = attn_layer(shift_tokens(x), Wqkv[i], q_scale[i], k_scale[i], Wo[i]) + x
            x = ffn_layer(shift_tokens(x), ln_g[i], ln_b[i], W1[i], b1[i], W2[i], b2[i]) + x
        return x
    x = L0_attn_x
    mod = (_silu(L0_c) @ L0_wmod).reshape(L0_c.shape[0], 6, 1, -1)
    sa, ca, ga, sb, cb, gb = (mod[:, 0], mod[:, 1], mod[:, 2], mod[:, 3], mod[:, 4], mod[:, 5])
    ga = (2 * (ga >= 0) - 1) * jnp.maximum(jnp.abs(ga), 0.25)
    gb = (2 * (gb >= 0) - 1) * jnp.maximum(jnp.abs(gb), 0.25)
    h = _layernorm(x, axis=-1) * (1 + ca) + sa
    x = x + ga * _L0_attn_ref(h, L0_attn_Wq, L0_attn_bq, L0_attn_Wk, L0_attn_bk, L0_attn_Wv, L0_attn_bv, L0_attn_Wo, L0_attn_bo)
    h = _layernorm(x, axis=-1) * (1 + cb) + sb
    x = x + gb * _L0_ffn_ref(h, L0_ffn_Wqkv, L0_ffn_q_scale, L0_ffn_k_scale, L0_ffn_Wo, L0_ffn_ln_g, L0_ffn_ln_b, L0_ffn_W1, L0_ffn_b1, L0_ffn_W2, L0_ffn_b2)
    return x

_drawn_inputs = setup_inputs


def setup_inputs(seed=0):
    import zlib

    import numpy as np

    out = dict(_drawn_inputs(seed))
    spreads = {'L0_attn_bq': (0.0, 0.8),
     'L0_attn_bk': (0.0, 2.0),
     'L0_attn_bv': (0.0, 0.344),
     'L0_attn_bo': (0.0, 0.324),
     'L0_ffn_q_scale': (1.0, 0.6),
     'L0_ffn_k_scale': (1.0, 0.6),
     'L0_ffn_ln_g': (1.0, 0.6),
     'L0_ffn_ln_b': (0.0, 0.8),
     'L0_ffn_b1': (0.0, 0.8),
     'L0_ffn_b2': (0.0, 0.654)}
    factors = {'L0_ffn_W1': 7.424, 'L0_ffn_W2': 7.292}
    for name, (base, spread) in spreads.items():
        noise = np.random.default_rng([zlib.crc32(name.encode()), seed]).standard_normal(out[name].shape)
        drawn = base * np.exp(spread * noise) if base else spread * noise
        out[name] = jnp.asarray(drawn.astype(out[name].dtype))
    for name, factor in factors.items():
        out[name] = (out[name] * factor).astype(out[name].dtype)
    return out
```

```python
import concourse.bass as bass
from concourse import mybir
from contextlib import ExitStack
import numpy as np

F32 = mybir.dt.float32
BF16 = mybir.dt.bfloat16
ALU = mybir.AluOpType
ACT = mybir.ActivationFunctionType
AX = mybir.AxisListType

B, S, D = 8, 512, 128
DEPTH = 6
HEADS, DH, W = 16, 64, 32
INNER = HEADS * DH
HID = int(D * 4 * 2 / 3)
P = 128
TPB = S // P
NT = B * TPB
NI = DEPTH * NT
NWIN = P // W
HC = [(0, 128), (128, 128), (256, HID - 256)]
NCH = 3 * INNER // 512
HH = HEADS // 2
EPS = 1e-5
MASKED = -1e30


def tables():
    half = np.arange(0, DH, 2, dtype=np.float32)
    inv_freq = (1.0 / 10000.0 ** (half / DH)).astype(np.float32)
    t = np.arange(S, dtype=np.float32)
    freqs = (t[:, None] * inv_freq[None, :]).astype(np.float32)
    freqs = np.concatenate([freqs, freqs], -1).astype(np.float64)
    base = (half + 0.4 * DH) / (1.4 * DH)
    power = (t - S // 2) / (W // 2)
    scale = base[None, :].astype(np.float64) ** power[:, None]
    scale = np.concatenate([scale, scale], -1)
    sign = np.where(np.arange(DH) < DH // 2, -1.0, 1.0)
    cos, sin = np.cos(freqs), np.sin(freqs) * sign
    c = np.stack([cos * scale * 8.0, cos / scale], 1)
    s = np.stack([sin * scale * 8.0, sin / scale], 1)
    c = c.reshape(TPB, P, 2, DH).transpose(1, 0, 2, 3)
    s = s.reshape(TPB, P, 2, DH).transpose(1, 0, 2, 3)
    i = np.arange(P) % W
    w = np.arange(P) // W
    j = np.arange(W)
    prev = np.where(j[None, :] >= i[:, None], 0.0, MASKED)
    own = np.where(j[None, :] <= i[:, None], 0.0, MASKED)
    first = np.where(w[:, None] == 0, MASKED, prev)
    m = np.stack([np.concatenate([prev, own], 1), np.concatenate([first, own], 1)], 1)
    return (np.ascontiguousarray(c, np.float32), np.ascontiguousarray(s, np.float32),
            np.ascontiguousarray(m, np.float32), np.eye(P, dtype=np.float32))


def wait(eng, sem, value):
    if type(value) is int and value <= 0:
        return
    eng.wait_ge(sem, value)


def adaln_block(nc, x_d, wq_d, wk_d, wv_d, wo_d, bq_d, bk_d, bv_d, bo_d, cT_d, wmod_d,
                wqkv_d, qs_d, ks_d, fwo_d, g_d, bln_d, w1_d, b1_d, w2_d, b2_d,
                tc_d, ts_d, mask_d, eye_d, out_d):
    ctx = ExitStack()
    with ctx:
        def sb(name, shape, dt=F32):
            return ctx.enter_context(nc.sbuf_tensor(name, shape, dt))

        def sem(name):
            return ctx.enter_context(nc.semaphore(name))

        X1 = sb("X1", [P, NT, D])
        Y = sb("Y", [P, NT, D])
        GB = sb("GB", [P, B, D])
        ident = sb("ident", [P, P])
        identb = sb("identb", [P, P], BF16)
        maskf = sb("maskf", [P, 2, DH])
        maskb = sb("maskb", [P, 2, HH, DH], BF16)
        TC = sb("TC", [P, DEPTH, TPB, 2, DH])
        TS = sb("TS", [P, DEPTH, TPB, 2, DH])
        qks = sb("qks", [P, DEPTH, 2, DH])
        aw = sb("aw", [P, 4, D])
        ab = sb("ab", [P, 4])
        cT = sb("cT", [P, B])
        sc = sb("sc", [P, 2, B])
        wmod = sb("wmod", [P, 6, D])
        modT = sb("modT", [P, 6, B])
        gt = sb("gt", [P, 2, B])
        cur = sb("cur", [P, 6])
        wqkv = sb("wqkv", [P, NCH, 512])
        fwo = sb("fwo", [P, INNER // P, D])
        w1 = sb("w1", [P, 2 * HID])
        w2 = sb("w2", [P, 3, D])
        fv = sb("fv", [P, 2])
        b1 = sb("b1", [P, 6])
        b2 = sb("b2", [1, D])
        ones = sb("ones", [1, P])
        nhalf = sb("nhalf", [P, 2 * HEADS])
        xp = sb("xp", [P, 2, D])
        xs = sb("xs", [P, 2, P + 1])
        raw = sb("raw", [P, 2 * INNER])
        rot = sb("rot", [P, 2 * INNER])
        swp = sb("swp", [P, 2 * INNER])
        ss = sb("ss", [P, 2 * HEADS])
        ssm = sb("ssm", [P, 2 * HEADS])
        rr = sb("rr", [P, 2 * HEADS])
        qT = sb("qT", [P, 2, HH, P])
        kT = sb("kT", [P, 2, HH, W + P])
        V = sb("V", [P, 2, INNER])
        Vp = sb("Vp", [P, 2, INNER])
        mx = sb("mx", [P, 2, HH])
        Pr = sb("Pr", [P, 2, 512])
        PT = sb("PT", [P, 2, 512])
        sm = sb("sm", [P, 2, HH])
        rs = sb("rs", [P, 2, HH])
        O = sb("O", [P, INNER])
        OT = sb("OT", [P, INNER // P, P])
        xf = sb("xf", [P, D])
        fs = sb("fs", [P, 2, P + 1])
        st = sb("st", [P, 6])
        mv = sb("mv", [P, 2])
        vpe = sb("vpe", [P, 1])
        rstd = sb("rstd", [P, 1])
        xn = sb("xn", [P, D])
        xnT = sb("xnT", [P, P])
        ge = sb("ge", [P, 3, P])
        hh = sb("hh", [P, 3, P])
        ax = raw[:, 0:512].rearrange("p (j f) -> p j f", j=TPB)
        an = raw[:, 512:1024].rearrange("p (j f) -> p j f", j=TPB)
        ah = raw[:, 1024:1536]
        a2 = raw[:, 1536:2048].rearrange("p (j f) -> p j f", j=TPB)
        aq = rot[:, 0:512]
        ak = rot[:, 512:1024]
        av = rot[:, 1024:1536].rearrange("p (j f) -> p j f", j=TPB)
        ao = rot[:, 1536:2048]
        apT = swp[:, :].rearrange("p (t s) -> p t s", t=TPB)
        ath = [qT[:, i, 0:4, :].rearrange("p a b -> p (a b)") for i in range(2)]
        ath2 = [qT[:, i, 4:8, :].rearrange("p a b -> p (a b)") for i in range(2)]
        are = [Pr[:, i, :] for i in range(2)]
        tcb = sb("tcb", [P, TPB, 2, DH])
        tsb = sb("tsb", [P, TPB, 2, DH])
        ast = sb("ast", [P, TPB, 6])
        amv = sb("amv", [P, TPB, 2])
        ave = sb("ave", [P, TPB])
        ars = sb("ars", [P, TPB])
        anm = sb("anm", [P, TPB])
        asum = sb("asum", [P, TPB])
        arc = sb("arc", [P, TPB])
        ay = PT[:, 0, :]
        ah2 = PT[:, 1, :]

        bank = [ctx.enter_context(nc.psum_tensor(f"bank{i}", [P, 512], F32)) for i in range(8)]

        ld_const = sem("ld_const")
        ld_attn = sem("ld_attn")
        ld_x = sem("ld_x")
        wq_loaded = [sem(f"wq_loaded{c}") for c in range(NCH)]
        fw_loaded = sem("fw_loaded")
        vp_moved = sem("vp_moved")
        out_stored = sem("out_stored")
        passed = sem("passed")
        silu_in = sem("silu_in")
        silu_mul = sem("silu_mul")
        mod_done = sem("mod_done")
        mod_ready = sem("mod_ready")
        ones_ready = sem("ones_ready")
        mask_ready = sem("mask_ready")
        silu_add = sem("silu_add")
        zero_ready = sem("zero_ready")
        a_stats = sem("a_stats")
        a_aggr = sem("a_aggr")
        a_var = sem("a_var")
        a_rstd = sem("a_rstd")
        a_norm = sem("a_norm")
        a_nT = sem("a_nT")
        a_cur = sem("a_cur")
        a_h = sem("a_h")
        a_proj = sem("a_proj")
        a_qs = sem("a_qs")
        a_ks = sem("a_ks")
        a_vs = sem("a_vs")
        a_score = sem("a_score")
        a_act = sem("a_act")
        a_theta1 = sem("a_theta1")
        a_theta = sem("a_theta")
        a_max = sem("a_max")
        a_exp = sem("a_exp")
        a_recip = sem("a_recip")
        a_prob = sem("a_prob")
        a_pT = sem("a_pT")
        a_pTs = sem("a_pTs")
        a_out = sem("a_out")
        a_outs = sem("a_outs")
        a_y = sem("a_y")
        a_ys = sem("a_ys")
        a_yT = sem("a_yT")
        a_x2 = sem("a_x2")
        a_x1 = sem("a_x1")
        a_back = sem("a_back")
        a_gb = sem("a_gb")
        y_ready = sem("y_ready")
        xp_ready = sem("xp_ready")
        xT_done = sem("xT_done")
        xs_ready = sem("xs_ready")
        xcol_ready = sem("xcol_ready")
        proj_done = sem("proj_done")
        proj_out = sem("proj_out")
        sq_ready = sem("sq_ready")
        ss_ready = sem("ss_ready")
        ssm_ready = sem("ssm_ready")
        rr_ready = sem("rr_ready")
        qn_ready = sem("qn_ready")
        cosp_ready = sem("cosp_ready")
        sinp_ready = sem("sinp_ready")
        rot_ready = sem("rot_ready")
        qkT_done = sem("qkT_done")
        qkT_out = sem("qkT_out")
        kprev_ready = sem("kprev_ready")
        score_done = sem("score_done")
        max_ready = sem("max_ready")
        sub_ready = sem("sub_ready")
        exp_ready = sem("exp_ready")
        sum_ready = sem("sum_ready")
        rsum_ready = sem("rsum_ready")
        pT_ready = sem("pT_ready")
        pv_done = sem("pv_done")
        o_ready = sem("o_ready")
        oT_done = sem("oT_done")
        oT_out = sem("oT_out")
        wo_done = sem("wo_done")
        xf_ready = sem("xf_ready")
        fT_done = sem("fT_done")
        fs_ready = sem("fs_ready")
        fcol_ready = sem("fcol_ready")
        fback_done = sem("fback_done")
        st_ready = sem("st_ready")
        mv_ready = sem("mv_ready")
        vpe_ready = sem("vpe_ready")
        rstd_ready = sem("rstd_ready")
        xn_ready = sem("xn_ready")
        xnT_done = sem("xnT_done")
        xnT_ready = sem("xnT_ready")
        gate_done = sem("gate_done")
        lin_done = sem("lin_done")
        ge_ready = sem("ge_ready")
        hh_ready = sem("hh_ready")
        w2_done = sem("w2_done")
        fin_mul = sem("fin_mul")
        fin_ready = sem("fin_ready")

        GROUPS = NI // TPB - 1

        def slots(eng, body):
            for g in range(TPB + 2):
                body(g, g, True, g >= 1, g >= 2)
            with eng.Fori(1, GROUPS) as k:
                for i in range(TPB):
                    body(k * TPB + (2 + i), 2 + i, True, True, True)
            for g in range(TPB * GROUPS + 2, NI + 2):
                body(g, g, g < NI, g < NI + 1, True)

        def batches(eng, body):
            body(0)
            with eng.Fori(1, B) as b:
                body(b)

        block = ctx.enter_context(nc.Block())
        FWL = 13 * 16
        CONST = (4 + 2 * DEPTH) * 16

        def layer(n):
            return n // NT

        def alone(eng):
            eng.sem_inc(passed, 1)

        @block.sync
        def _(sp):
            for dst, src in ((ident[:, :], eye_d), (maskf[:, :, :], mask_d),
                             (tcb[:, :, :, :], tc_d), (tsb[:, :, :, :], ts_d)):
                sp.dma_start(dst, src).then_inc(ld_const, 16)
            for l in range(DEPTH):
                for i, s_d in enumerate((qs_d, ks_d)):
                    sp.dma_start(qks[:, l, i, :], s_d[l:l + 1, :].broadcast_to([P, DH])).then_inc(ld_const, 16)
            for i, w_d in enumerate((wq_d, wk_d, wv_d, wo_d)):
                sp.dma_start(aw[:, i, :], w_d).then_inc(ld_attn, 16)
            for i, b_d in enumerate((bq_d, bk_d, bv_d, bo_d)):
                sp.dma_start(ab[:, i:i + 1], b_d).then_inc(ld_attn, 16)
            sp.dma_start(cT[:, :], cT_d).then_inc(ld_attn, 16)
            sp.dma_start(wmod[:, :, :], wmod_d).then_inc(ld_attn, 16)
            for b in range(B):
                wait(sp, a_x2, b)
                wait(sp, a_yT, b)
                sp.dma_start(ax, x_d[b].rearrange("(j p) f -> p j f", p=P)).then_inc(ld_x, 16)

            def shift_v(n, par):
                sp.wait_ge(proj_out, n * NCH + NCH)
                alone(sp)
                wait(sp, vp_moved, n * 32)
                wait(sp, pv_done, n * 2 - 2)
                sp.dma_start(Vp[W:P, par, :], V[0:P - W, par, :]).then_inc(vp_moved, 16)
                sp.dma_start(Vp[0:W, par, :], V[P - W:P, 1 - par, :]).then_inc(vp_moved, 16)

            def loads_and_moves(l):
                for c in range(NCH):
                    wait(sp, proj_done, l * (NT * NCH))
                    alone(sp)
                    sp.dma_start(wqkv[:, c, :], wqkv_d[l, :, c * 512:(c + 1) * 512]).then_inc(wq_loaded[c], 16)
                for j in range(2):
                    shift_v(l * NT + j, j % 2)
                wait(sp, w2_done, l * NT)
                alone(sp)
                sp.dma_start(fwo[:, :, :], fwo_d[l].rearrange("(c p) n -> p c n", p=P)).then_inc(fw_loaded, 16)
                sp.dma_start(w1[:, :], w1_d[l]).then_inc(fw_loaded, 16)
                sp.dma_start(w2[:, 0:2, :], w2_d[l, 0:256, :].rearrange("(c p) n -> p c n", p=P)).then_inc(fw_loaded, 16)
                sp.dma_start(w2[0:HID - 256, 2, :], w2_d[l, 256:HID, :]).then_inc(fw_loaded, 16)
                sp.dma_start(fv[:, 0:1], g_d[l]).then_inc(fw_loaded, 16)
                sp.dma_start(fv[:, 1:2], bln_d[l]).then_inc(fw_loaded, 16)
                for i in range(2):
                    for c, (h0, hn) in enumerate(HC):
                        sp.dma_start(b1[0:hn, 3 * i + c:3 * i + c + 1],
                                     b1_d[l, i * HID + h0:i * HID + h0 + hn, :]).then_inc(fw_loaded, 16)
                sp.dma_start(b2[:, :], b2_d[l]).then_inc(fw_loaded, 16)
                for j in range(2, TPB):
                    shift_v(l * NT + j, j % 2)
                with sp.Fori(1, B) as b:
                    for j in range(TPB):
                        shift_v(l * NT + b * TPB + j, j % 2)

            loads_and_moves(0)
            with sp.Fori(1, DEPTH) as l:
                loads_and_moves(l)
            for b in range(B):
                sp.wait_ge(fin_ready, b + 1)
                sp.dma_start(out_d[b].rearrange("(j p) f -> p j f", p=P),
                             Y[:, b * TPB:(b + 1) * TPB, :]).then_inc(out_stored, 16)
            sp.wait_ge(out_stored, 16 * B)

        @block.tensor
        def _(pe):
            pe.wait_ge(ld_attn, 160)
            pe.wait_ge(silu_mul, 1)
            for i in range(6):
                mm = nc.tensor.matmul(bank[0][:, i * B:(i + 1) * B], wmod[:, i, :], sc[:, 1, :], start=True, stop=True)
            mm.then_inc(mod_done, 1)
            pe.wait_ge(ld_const, CONST)
            pe.wait_ge(mod_ready, 1)

            def first_attention(b):
                wait(pe, a_norm, 2 * b + 1)
                wait(pe, a_outs, b)
                wait(pe, a_h, 2 * b)
                for j in range(TPB):
                    mm = nc.tensor.transpose(bank[0][:, j * P:(j + 1) * P], an[:, j, :], ident[:, :])
                mm.then_inc(a_nT, 1)
                wait(pe, a_h, 2 * b + 1)
                wait(pe, y_ready, TPB * b)
                wait(pe, a_gb, b)
                nc.tensor.matmul(bank[1][:, :], aw[:, 0, :], ah, start=True, stop=True).then_inc(a_proj, 1)
                nc.tensor.matmul(bank[2][:, :], aw[:, 1, :], ah, start=True, stop=True).then_inc(a_proj, 1)
                for j in range(TPB):
                    mm = nc.tensor.matmul(bank[3][:, j * P:(j + 1) * P], ah[:, j * P:(j + 1) * P], aw[:, 2, :],
                                          start=True, stop=True)
                mm.then_inc(a_proj, 1)
                wait(pe, a_qs, b + 1)
                wait(pe, a_ks, b + 1)
                for j in range(TPB):
                    nc.tensor.matmul(bank[4 + j][:, :], aq[:, j * P:(j + 1) * P], ak, start=True, stop=True)\
                        .then_inc(a_score, 1)
                for j in range(TPB):
                    wait(pe, a_prob, TPB * b + j + 1)
                    for u in range(TPB):
                        mm = nc.tensor.transpose(bank[4 + j][:, u * P:(u + 1) * P], are[j % 2][:, u * P:(u + 1) * P],
                                                 ident[:, :])
                    mm.then_inc(a_pT, 1)
                wait(pe, a_pTs, TPB * (b + 1))
                wait(pe, a_vs, b + 1)
                for u in range(TPB):
                    mm = nc.tensor.matmul(bank[0][:, :], av[:, u, :], apT[:, u, :], start=(u == 0), stop=(u == TPB - 1))
                mm.then_inc(a_out, 1)
                wait(pe, a_outs, b + 1)
                nc.tensor.matmul(bank[1][:, :], aw[:, 3, :], ao, start=True, stop=True).then_inc(a_y, 1)
                wait(pe, a_ys, b + 1)
                for j in range(TPB):
                    mm = nc.tensor.transpose(bank[2][:, j * P:(j + 1) * P], ay[:, j * P:(j + 1) * P], ident[:, :])
                mm.then_inc(a_yT, 1)
                wait(pe, a_norm, 2 * b + 2)
                for j in range(TPB):
                    mm = nc.tensor.transpose(bank[0][:, j * P:(j + 1) * P], an[:, j, :], ident[:, :])
                mm.then_inc(a_nT, 1)
                nc.tensor.matmul(bank[3][:, 0:P], cur[:, 5:6].broadcast_to([P, P]), ident[:, :], start=True, stop=True)
                wait(pe, a_h, 2 * b + 2)
                for j in range(TPB):
                    mm = nc.tensor.transpose(bank[1][:, j * P:(j + 1) * P], ah2[:, j * P:(j + 1) * P], ident[:, :])
                mm.then_inc(a_back, 1)

            batches(pe, first_attention)

            def scores(a, par, j, h):
                if h == 0:
                    pe.wait_ge(qkT_out, 4 * a + 4)
                    pe.wait_ge(kprev_ready, a + 1)
                    wait(pe, o_ready, 2 * a)
                nc.tensor.matmul(bank[3 + h][:, :], identb[:, :],
                                 maskb[:, 1 if j == 0 else 0, :, :].rearrange("p h k -> p (h k)"),
                                 start=True, stop=False, skip_group_check=True)
                r = slice(h * DH, (h + 1) * DH)
                for w in range(NWIN):
                    for u in range(HH):
                        mm = nc.tensor.matmul(bank[3 + h][w * W:(w + 1) * W, u * DH:(u + 1) * DH],
                                              qT[r, par, u, w * W:(w + 1) * W],
                                              kT[r, par, u, w * W:w * W + 2 * W],
                                              start=False, stop=True, skip_group_check=True)
                mm.then_inc(score_done, 1)

            def pv(a, par, h):
                pe.wait_ge(pT_ready, 2 * a + h + 1)
                pe.wait_ge(proj_out, NCH * a + NCH)
                pe.wait_ge(vp_moved, 32 * a + 32)
                alone(pe)
                bk = bank[5] if h == 0 else bank[3]
                for u in range(HH):
                    hc = (2 * u + h) * DH
                    for w in range(NWIN):
                        r = slice(w * W, (w + 1) * W)
                        nc.tensor.matmul(bk[r, u * DH:(u + 1) * DH], PT[r, h, u * 2 * W:u * 2 * W + W],
                                         Vp[r, par, hc:hc + DH], start=True, stop=False)
                        mm = nc.tensor.matmul(bk[r, u * DH:(u + 1) * DH], PT[r, h, u * 2 * W + W:(u + 1) * 2 * W],
                                              V[r, par, hc:hc + DH], start=False, stop=True)
                mm.then_inc(pv_done, 1)

            def qk_back(n, i):
                pe.wait_ge(rot_ready, 2 * n + i // 2 + 1)
                if i == 3:
                    pe.wait_ge(qkT_out, 4 * n + 1)
                if i == 2:
                    wait(pe, o_ready, 2 * n - 1)
                bk = bank[[2, 4, 5, 2][i]]
                for u in range(4):
                    col = (4 * i + u) * P
                    mm = nc.tensor.transpose(bk[:, u * P:(u + 1) * P], rot[:, col:col + P], ident[:, :])
                mm.then_inc(qkT_done, 1)

            def slot(g, gs, do_p, do_a, do_f):
                n, a, u = g, g - 1, g - 2
                par = gs % 2
                ja = (gs - 1) % TPB
                if do_p:
                    pe.wait_ge(xp_ready, n + 1)
                    wait(pe, qkT_out, 4 * n)
                    nc.tensor.transpose(bank[2][:, 0:P], xp[:, par, :], ident[:, :]).then_inc(xT_done, 1)
                if do_f:
                    pe.wait_ge(o_ready, 2 * u + 2)
                    pe.wait_ge(y_ready, NT + u)
                    for i in range(2):
                        for c in range(4):
                            mm = nc.tensor.transpose(bank[6 + i][:, c * P:(c + 1) * P],
                                                     O[:, (4 * i + c) * P:(4 * i + c + 1) * P], ident[:, :])
                        mm.then_inc(oT_done, 1)
                if do_a:
                    scores(a, 1 - par, ja, 0)
                if do_p:
                    pe.wait_ge(xs_ready, n + 1)
                    pe.wait_ge(xcol_ready, n + 1)
                    pproj(n, 0, par)
                if do_f:
                    pe.wait_ge(oT_out, 2 * u + 2)
                    pe.wait_ge(fw_loaded, layer(u) * FWL + FWL)
                    for c in range(INNER // P):
                        mm = nc.tensor.matmul(bank[6][:, 0:P], OT[:, c, :], fwo[:, c, :],
                                              start=(c == 0), stop=(c == INNER // P - 1))
                    mm.then_inc(wo_done, 1)
                if do_a:
                    scores(a, 1 - par, ja, 1)
                if do_p:
                    pproj(n, 1, par)
                if do_f:
                    pe.wait_ge(xf_ready, u + 1)
                    nc.tensor.transpose(bank[7][:, 0:P], xf[:, :], ident[:, :]).then_inc(fT_done, 1)
                if do_p:
                    pproj(n, 2, par)
                if do_f:
                    pe.wait_ge(fs_ready, u + 1)
                    pe.wait_ge(fcol_ready, u + 1)
                    nc.tensor.transpose(bank[6][:, 0:P], fs[:, par, 0:P], ident[:, :]).then_inc(fback_done, 1)
                if do_p:
                    pproj(n, 3, par)
                if do_a:
                    pv(a, 1 - par, 0)
                if do_f:
                    pe.wait_ge(xn_ready, u + 1)
                    nc.tensor.transpose(bank[7][:, 0:P], xn[:, :], ident[:, :]).then_inc(xnT_done, 1)
                if do_a:
                    pv(a, 1 - par, 1)
                if do_f:
                    pe.wait_ge(xnT_ready, u + 1)
                    for i, bk, done in ((1, bank[7], gate_done), (0, bank[6], lin_done)):
                        for c, (h0, hn) in enumerate(HC):
                            mm = nc.tensor.matmul(bk[0:hn, c * P:(c + 1) * P], w1[:, i * HID + h0:i * HID + h0 + hn],
                                                  xnT[:, :], start=True, stop=True)
                        mm.then_inc(done, 1)
                if do_p:
                    pproj(n, 4, par)
                    pproj(n, 5, par)
                if do_f:
                    pe.wait_ge(hh_ready, u + 1)
                    for c, (h0, hn) in enumerate(HC):
                        nc.tensor.matmul(bank[6][:, 0:P], hh[0:hn, c, :], w2[0:hn, c, :], start=(c == 0), stop=False)
                    nc.tensor.matmul(bank[6][:, 0:P], ones[:, :], b2[:, :], start=False, stop=True).then_inc(w2_done, 1)
                if do_p:
                    for i in range(4):
                        qk_back(n, i)

            def pproj(n, c, par):
                wait(pe, proj_out, n * NCH + (c - 1))
                pe.wait_ge(wq_loaded[c], layer(n) * 16 + 16)
                nc.tensor.matmul(bank[c % 2][:, :], xs[:, par, 0:P], wqkv[:, c, :], start=True, stop=True)\
                    .then_inc(proj_done, 1)

            pe.wait_ge(ones_ready, 1)
            pe.wait_ge(mask_ready, 1)
            pe.wait_ge(a_gb, B)
            slots(pe, slot)

        @block.scalar
        def _(act):
            act.wait_ge(ld_attn, 160)
            nc.scalar.activation(sc[:, 0, :], cT[:, :], ACT.Tanh, scale=0.5).then_inc(silu_in, 1)

            def theta_parts(b, j):
                wait(act, a_score, TPB * b + j + 1)
                wait(act, a_theta, TPB * b + j - 1 if j >= 2 else TPB * b)
                wait(act, a_pT, TPB * b + j - 1 if j >= 2 else TPB * b)
                nc.scalar.activation(ath[j % 2], bank[4 + j][:, :], ACT.Tanh, scale=0.5)
                nc.scalar.activation(ath2[j % 2], bank[4 + j][:, :], ACT.Tanh)
                nc.scalar.activation(are[j % 2], bank[4 + j][:, :], ACT.Relu, scale=0.1).then_inc(a_act, 1)

            def exps(b, j):
                wait(act, a_max, TPB * b + j + 1)
                nc.scalar.activation(are[j % 2], are[j % 2], ACT.Exp, bias=anm[:, j:j + 1],
                                     accum_out=asum[:, j:j + 1]).then_inc(a_exp, 1)

            def probs_out(b, j):
                wait(act, a_pT, TPB * b + j + 1)
                nc.scalar.activation(apT[:, :, j * P:(j + 1) * P],
                                     bank[4 + j][:, :].rearrange("p (u s) -> p u s", u=TPB), ACT.Copy)\
                    .then_inc(a_pTs, 1)

            def first_attention(b):
                wait(act, a_nT, 2 * b + 1)
                wait(act, a_cur, b + 1)
                wait(act, a_proj, 3 * b)
                nc.scalar.activation(ah, bank[0][:, :], ACT.Identity, scale=cur[:, 1:2], bias=cur[:, 0:1]).then_inc(a_h, 1)
                wait(act, a_proj, 3 * b + 2)
                nc.scalar.activation(ak, bank[2][:, :], ACT.Identity, bias=ab[:, 1:2], scale=1.0).then_inc(a_ks, 1)
                wait(act, a_out, b)
                theta_parts(b, 0)
                theta_parts(b, 1)
                exps(b, 0)
                exps(b, 1)
                probs_out(b, 0)
                theta_parts(b, 2)
                probs_out(b, 1)
                theta_parts(b, 3)
                exps(b, 2)
                exps(b, 3)
                probs_out(b, 2)
                probs_out(b, 3)
                wait(act, a_nT, 2 * b + 2)
                wait(act, a_back, b)
                nc.scalar.activation(ah2, bank[0][:, :], ACT.Identity, scale=cur[:, 4:5], bias=cur[:, 3:4]).then_inc(a_h, 1)

            batches(act, first_attention)

            def to_raw(n, c):
                act.wait_ge(proj_done, NCH * n + c + 1)
                if c == 0:
                    wait(act, sinp_ready, 2 * n)
                    wait(act, cosp_ready, 2 * n)
                nc.scalar.activation(raw[:, c * 512:(c + 1) * 512], bank[c % 2][:, :], ACT.Copy).then_inc(proj_out, 1)

            def squares(n, i):
                act.wait_ge(proj_out, NCH * n + 2 * i + 2)
                wait(act, qkT_done, 4 * n)
                nc.scalar.activation(rot[:, i * INNER:(i + 1) * INNER], raw[:, i * INNER:(i + 1) * INNER],
                                     ACT.Square).then_inc(sq_ready, 1)

            def to_v(n, par, c):
                act.wait_ge(proj_done, NCH * n + c + 1)
                if c == 4:
                    wait(act, pv_done, 2 * n - 2)
                    wait(act, vp_moved, 32 * n)
                nc.scalar.activation(V[:, par, (c - 4) * 512:(c - 3) * 512], bank[c % 2][:, :], ACT.Copy)\
                    .then_inc(proj_out, 1)

            def exp_half(a, h):
                act.wait_ge(sub_ready, 2 * a + h + 1)
                nc.scalar.activation(Pr[:, h, :], Pr[:, h, :], ACT.Exp).then_inc(exp_ready, 1)

            def slot(g, gs, do_p, do_a, do_f):
                n, a, u, par = g, g - 1, g - 2, gs % 2
                if do_p:
                    act.wait_ge(xT_done, n + 1)
                    wait(act, xcol_ready, n)
                    nc.scalar.activation(xs[0:64, par, 0:P], bank[2][0:64, 0:P], ACT.Copy)
                    nc.scalar.activation(xs[64:P, par, 1:P + 1], bank[2][64:P, 0:P], ACT.Copy).then_inc(xs_ready, 1)
                if do_f:
                    for i in range(2):
                        act.wait_ge(oT_done, 2 * u + i + 1)
                        wait(act, wo_done, u)
                        nc.scalar.activation(OT[:, 4 * i:4 * i + 4, :], bank[6 + i][:, :].rearrange("p (c s) -> p c s", c=4),
                                             ACT.Copy).then_inc(oT_out, 1)
                if do_p:
                    to_raw(n, 0)
                if do_a:
                    exp_half(a, 0)
                if do_p:
                    to_raw(n, 1)
                    squares(n, 0)
                if do_f:
                    act.wait_ge(fT_done, u + 1)
                    wait(act, fcol_ready, u)
                    nc.scalar.activation(fs[0:64, par, 0:P], bank[7][0:64, 0:P], ACT.Copy)
                    nc.scalar.activation(fs[64:P, par, 1:P + 1], bank[7][64:P, 0:P], ACT.Copy).then_inc(fs_ready, 1)
                if do_p:
                    to_raw(n, 2)
                if do_a:
                    exp_half(a, 1)
                if do_p:
                    to_raw(n, 3)
                    squares(n, 1)
                if do_f:
                    act.wait_ge(xnT_done, u + 1)
                    nc.scalar.activation(xnT[:, :], bank[7][:, 0:P], ACT.Identity, scale=fv[:, 0:1], bias=fv[:, 1:2])\
                        .then_inc(xnT_ready, 1)
                    act.wait_ge(gate_done, u + 1)
                    wait(act, hh_ready, u)
                    for c, (h0, hn) in enumerate(HC):
                        last = nc.scalar.activation(ge[0:hn, c, :], bank[7][0:hn, c * P:(c + 1) * P], ACT.Gelu,
                                                    bias=b1[0:hn, 3 + c:4 + c], scale=1.0)
                    last.then_inc(ge_ready, 1)
                if do_p:
                    to_v(n, par, 4)
                    to_v(n, par, 5)
                    for i in range(4):
                        act.wait_ge(qkT_done, 4 * n + i + 1)
                        src = bank[[2, 4, 5, 2][i]][:, :].rearrange("p (c s) -> p c s", c=4)
                        if i < 2:
                            dst = qT[:, par, 4 * i:4 * i + 4, :]
                        else:
                            wait(act, kprev_ready, n)
                            dst = kT[:, par, 4 * i - 8:4 * i - 4, W:W + P]
                        wait(act, score_done, 2 * n - 2)
                        nc.scalar.activation(dst, src, ACT.Copy).then_inc(qkT_out, 1)

            slots(act, slot)

        @block.gpsimd
        def _(pool):
            pool.memset(ones[:, :], 1.0)
            pool.memset(nhalf[:, :], -0.5).then_inc(ones_ready, 1)
            pool.memset(kT[:, :, :, :], 0.0)
            pool.memset(V[:, :, :], 0.0).then_inc(zero_ready, 1)
            pool.wait_ge(ones_ready, 1)
            pool.wait_ge(ld_const, CONST)
            for l in range(DEPTH):
                for j in range(TPB):
                    pool.tensor_tensor(TC[:, l, j, :, :], tcb[:, j, :, :], qks[:, l, :, :], ALU.mult)
                    pool.tensor_tensor(TS[:, l, j, :, 0:32], tsb[:, j, :, 0:32], qks[:, l, :, 32:64], ALU.mult)
                    pool.tensor_tensor(TS[:, l, j, :, 32:64], tsb[:, j, :, 32:64], qks[:, l, :, 0:32], ALU.mult)\
                        .then_inc(zero_ready, 1)

            pool.wait_ge(mod_ready, 1)

            def first_attention(b):
                def rstd4(i):
                    wait(pool, a_aggr, 2 * b + i + 1)
                    wait(pool, a_norm, 2 * b + i)
                    alone(pool)
                    pool.tensor_scalar(ave[:, :], amv[:, :, 1], EPS, None, ALU.add).then_inc(a_var, 1)
                    wait(pool, a_var, 2 * b + i + 1)
                    pool.tensor_tensor(ars[:, :], ave[:, :], nhalf[:, 0:TPB], ALU.pow).then_inc(a_rstd, 1)
                wait(pool, a_back, b)
                wait(pool, a_ys, b)
                wait(pool, a_h, 2 * b)
                alone(pool)
                pool.tensor_copy(cur[:, :].unsqueeze(2), modT[:, :, bass.ds(b, 1)]).then_inc(a_cur, 1)
                rstd4(0)
                wait(pool, a_x2, b + 1)
                alone(pool)
                pool.tensor_copy(X1[:, bass.ds(b * TPB, TPB), :], a2).then_inc(a_x1, 1)
                rstd4(1)

            batches(pool, first_attention)

            def norms(n, i):
                s = slice(i * HEADS, (i + 1) * HEADS)
                pool.wait_ge(ss_ready, 2 * n + i + 1)
                wait(pool, qn_ready, 2 * n)
                alone(pool)
                pool.tensor_scalar(ssm[:, s], ss[:, s], 1e-24, None, ALU.max).then_inc(ssm_ready, 1)
                pool.wait_ge(ssm_ready, 2 * n + i + 1)
                pool.tensor_tensor(rr[:, s], ssm[:, s], nhalf[:, s], ALU.pow).then_inc(rr_ready, 1)

            def sin_part(n, gs, i):
                pool.wait_ge(qn_ready, 2 * n + i + 1)
                wait(pool, rot_ready, 2 * n)
                src = raw[:, i * INNER:(i + 1) * INNER].rearrange("p (h t d) -> p h t d", t=2, d=32)
                dst = swp[:, i * INNER:(i + 1) * INNER].rearrange("p (h t d) -> p h t d", t=2, d=32)
                for t in range(2):
                    tab = TS[:, bass.ds(layer(n), 1), gs % TPB, i, 32 * t:32 * t + 32]
                    last = pool.tensor_tensor(dst[:, :, t, :], src[:, :, 1 - t, :],
                                              tab.broadcast_to([P, HEADS, 32]), ALU.mult)
                last.then_inc(sinp_ready, 1)

            def slot(g, gs, do_p, do_a, do_f):
                n, a, u, par = g, g - 1, g - 2, gs % 2
                if do_p:
                    pool.wait_ge(y_ready, n + 1)
                    wait(pool, xT_done, n - 1)
                    alone(pool)
                    pool.tensor_copy(xp[:, par, :].unsqueeze(1), Y[:, bass.ds(n % NT, 1), :]).then_inc(xp_ready, 1)
                    wait(pool, proj_done, NCH * (n - 1))
                    wait(pool, xs_ready, n)
                    pool.wait_ge(xp_ready, n + 1)
                    alone(pool)
                    if gs % TPB == 0:
                        alone(pool)
                        pool.memset(xs[64:P, par, 0:1], 0.0).then_inc(xcol_ready, 1)
                    else:
                        alone(pool)
                        pool.tensor_copy(xs[64:P, par, 0:1], xs[64:P, 1 - par, P:P + 1]).then_inc(xcol_ready, 1)
                    pool.wait_ge(xcol_ready, n + 1)
                    norms(n, 0)
                if do_f:
                    if do_p:
                        pool.wait_ge(rr_ready, 2 * n + 1)
                    else:
                        pool.wait_ge(kprev_ready, NI)
                    wait(pool, xn_ready, u)
                    wait(pool, fs_ready, u)
                    if (gs - 2) % TPB == 0:
                        alone(pool)
                        pool.memset(fs[64:P, par, 0:1], 0.0).then_inc(fcol_ready, 1)
                    else:
                        alone(pool)
                        pool.tensor_copy(fs[64:P, par, 0:1], fs[64:P, 1 - par, P:P + 1]).then_inc(fcol_ready, 1)
                    pool.wait_ge(fcol_ready, u + 1)
                    pool.wait_ge(mv_ready, u + 1)
                    alone(pool)
                    pool.tensor_scalar(vpe[:, :], mv[:, 1:2], EPS, None, ALU.add).then_inc(vpe_ready, 1)
                    pool.wait_ge(vpe_ready, u + 1)
                    pool.tensor_tensor(rstd[:, :], vpe[:, :], nhalf[:, 0:1], ALU.pow).then_inc(rstd_ready, 1)
                if do_p:
                    sin_part(n, gs, 0)
                    norms(n, 1)
                    sin_part(n, gs, 1)
                    wait(pool, qkT_out, 4 * n)
                    wait(pool, score_done, 2 * n - 2)
                    alone(pool)
                    pool.tensor_copy(kT[:, par, :, 0:W], kT[:, 1 - par, :, P:P + W]).then_inc(kprev_ready, 1)

            pool.wait_ge(a_x1, B)
            pool.wait_ge(zero_ready, 1 + DEPTH * TPB)
            slots(pool, slot)

        @block.vector
        def _(dve):
            dve.wait_ge(ld_const, CONST)
            nc.vector.tensor_copy(identb[:, :], ident[:, :])
            for h in range(HH):
                last = nc.vector.tensor_copy(maskb[:, :, h, :], maskf[:, :, :])
            last.then_inc(mask_ready, 1)
            dve.wait_ge(ld_attn, 160)
            dve.wait_ge(silu_in, 1)
            nc.vector.scalar_tensor_tensor(out=sc[:, 1, :], in0=sc[:, 0, :], scalar=1.0, in1=cT[:, :],
                                           op0=ALU.add, op1=ALU.mult).then_inc(silu_add, 1)
            dve.wait_ge(silu_add, 1)
            nc.vector.tensor_scalar(sc[:, 1, :], sc[:, 1, :], 0.5, None, ALU.mult).then_inc(silu_mul, 1)
            dve.wait_ge(mod_done, 1)
            mod = bank[0][:, 0:6 * B].rearrange("p (i b) -> p i b", i=6)
            for i in (0, 3):
                nc.vector.tensor_copy(modT[:, i, :], mod[:, i, :])
            for i in (1, 4):
                nc.vector.tensor_scalar(modT[:, i, :], mod[:, i, :], 1.0, None, ALU.add)
            for k, i in enumerate((2, 5)):
                nc.vector.tensor_scalar(gt[:, k, :], mod[:, i, :], 0.0, 2.0, ALU.is_ge, ALU.mult).then_inc(silu_mul, 1)
            dve.wait_ge(silu_mul, 3)
            for k, i in enumerate((2, 5)):
                nc.vector.scalar_tensor_tensor(out=modT[:, i, :], in0=gt[:, k, :], scalar=1.0, in1=mod[:, i, :],
                                               op0=ALU.subtract, op1=ALU.mult).then_inc(silu_mul, 1)
            dve.wait_ge(silu_mul, 5)
            for k, i in enumerate((2, 5)):
                nc.vector.tensor_scalar(modT[:, i, :], modT[:, i, :], 0.25, None, ALU.max).then_inc(silu_mul, 1)
            dve.wait_ge(silu_mul, 7)
            for k, i in enumerate((2, 5)):
                last = nc.vector.scalar_tensor_tensor(out=modT[:, i, :], in0=gt[:, k, :], scalar=1.0,
                                                      in1=modT[:, i, :], op0=ALU.subtract, op1=ALU.mult)
            last.then_inc(mod_ready, 1)

            def layernorm4(b, i, src):
                wait(dve, a_norm, 2 * b + i)
                for j in range(TPB):
                    last = nc.vector.bn_stats(ast[:, j, :], src[:, j, :])
                last.then_inc(a_stats, 1)
                wait(dve, a_stats, 2 * b + i + 1)
                wait(dve, a_rstd, 2 * b + i)
                alone(dve)
                for j in range(TPB):
                    last = nc.vector.bn_aggr(amv[:, j, :], ast[:, j, :])
                last.then_inc(a_aggr, 1)
                wait(dve, a_rstd, 2 * b + i + 1)
                wait(dve, a_aggr, 2 * b + i + 1)
                wait(dve, a_nT, 2 * b + i)
                for j in range(TPB):
                    last = nc.vector.tensor_scalar(an[:, j, :], src[:, j, :], amv[:, j, 0:1], ars[:, j:j + 1],
                                                   ALU.subtract, ALU.mult)
                last.then_inc(a_norm, 1)

            def theta(b, j):
                wait(dve, a_act, TPB * b + j + 1)
                nc.vector.scalar_tensor_tensor(out=are[j % 2], in0=ath[j % 2], scalar=0.1, in1=are[j % 2],
                                               op0=ALU.mult, op1=ALU.add).then_inc(a_theta1, 1)
                wait(dve, a_theta1, TPB * b + j + 1)
                nc.vector.scalar_tensor_tensor(out=are[j % 2], in0=ath2[j % 2], scalar=0.15, in1=are[j % 2],
                                               op0=ALU.mult, op1=ALU.add).then_inc(a_theta, 1)
                wait(dve, a_theta, TPB * b + j + 1)
                wait(dve, a_exp, TPB * b)
                nc.vector.tensor_reduce(anm[:, j:j + 1], are[j % 2], AX.X, ALU.max, negate=True).then_inc(a_max, 1)

            def probs(b, j):
                wait(dve, a_exp, TPB * b + j + 1)
                wait(dve, a_prob, TPB * b)
                nc.vector.reciprocal(arc[:, j:j + 1], asum[:, j:j + 1]).then_inc(a_recip, 1)
                wait(dve, a_recip, TPB * b + j + 1)
                nc.vector.tensor_scalar(are[j % 2], are[j % 2], arc[:, j:j + 1], None, ALU.mult).then_inc(a_prob, 1)

            def first_attention(b):
                wait(dve, ld_x, 16 * b + 16)
                layernorm4(b, 0, ax)
                wait(dve, a_proj, 3 * b + 1)
                wait(dve, a_score, TPB * b)
                nc.vector.tensor_scalar(aq, bank[1][:, :], ab[:, 0:1], None, ALU.add).then_inc(a_qs, 1)
                wait(dve, a_proj, 3 * b + 3)
                wait(dve, a_out, b)
                nc.vector.tensor_copy(av, bank[3][:, :].rearrange("p (j f) -> p j f", j=TPB)).then_inc(a_vs, 1)
                theta(b, 0)
                theta(b, 1)
                probs(b, 0)
                probs(b, 1)
                theta(b, 2)
                theta(b, 3)
                probs(b, 2)
                probs(b, 3)
                wait(dve, a_out, b + 1)
                wait(dve, a_y, b)
                nc.vector.tensor_scalar(ao, bank[0][:, :], ab[:, 2:3], None, ALU.add).then_inc(a_outs, 1)
                wait(dve, a_y, b + 1)
                wait(dve, a_yT, b)
                wait(dve, a_cur, b + 1)
                nc.vector.tensor_scalar(ay, bank[1][:, :], ab[:, 3:4], cur[:, 2:3], ALU.add, ALU.mult).then_inc(a_ys, 1)
                wait(dve, a_yT, b + 1)
                wait(dve, a_x1, b)
                nc.vector.tensor_tensor(a2, bank[2][:, :].rearrange("p (j f) -> p j f", j=TPB), ax, ALU.add)\
                    .then_inc(a_x2, 1)
                wait(dve, a_x2, b + 1)
                layernorm4(b, 1, a2)
                wait(dve, a_back, b + 1)
                nc.vector.tensor_copy(Y[:, bass.ds(b * TPB, TPB), :], bank[1][:, :].rearrange("p (j f) -> p j f", j=TPB))\
                    .then_inc(y_ready, TPB)
                nc.vector.tensor_copy(GB[:, bass.ds(b, 1), :], bank[3][:, 0:P].unsqueeze(1)).then_inc(a_gb, 1)

            batches(dve, first_attention)

            def maxes(a, h):
                dve.wait_ge(score_done, 2 * a + h + 1)
                wait(dve, sub_ready, 2 * a)
                nc.vector.tensor_reduce(mx[:, h, :], bank[3 + h][:, :].rearrange("p (u k) -> p u k", u=HH),
                                        AX.X, ALU.max).then_inc(max_ready, 1)
                dve.wait_ge(max_ready, 2 * a + h + 1)
                wait(dve, pT_ready, 2 * a)
                nc.vector.tensor_tensor(Pr[:, h, :].rearrange("p (u k) -> p u k", u=HH),
                                        bank[3 + h][:, :].rearrange("p (u k) -> p u k", u=HH),
                                        mx[:, h, :].unsqueeze(2).broadcast_to([P, HH, 2 * W]), ALU.subtract)\
                    .then_inc(sub_ready, 1)

            def sums(a, h):
                dve.wait_ge(exp_ready, 2 * a + h + 1)
                wait(dve, rsum_ready, 2 * a)
                nc.vector.tensor_reduce(sm[:, h, :], Pr[:, h, :].rearrange("p (u k) -> p u k", u=HH),
                                        AX.X, ALU.add).then_inc(sum_ready, 1)
                wait(dve, pv_done, 2 * a)
                nc.vector.transpose(PT[:, h, :], Pr[:, h, :]).then_inc(pT_ready, 1)
                dve.wait_ge(sum_ready, 2 * a + h + 1)
                wait(dve, o_ready, 2 * a)
                nc.vector.reciprocal(rs[:, h, :], sm[:, h, :]).then_inc(rsum_ready, 1)

            def outputs(a, h):
                dve.wait_ge(pv_done, 2 * a + h + 1)
                dve.wait_ge(rsum_ready, 2 * a + h + 1)
                wait(dve, oT_done, 2 * a)
                bk = bank[5] if h == 0 else bank[3]
                nc.vector.tensor_tensor(O[:, :].rearrange("p (u t d) -> p t u d", t=2, d=DH)[:, h, :, :],
                                        bk[:, :].rearrange("p (u k) -> p u k", u=HH),
                                        rs[:, h, :].unsqueeze(2).broadcast_to([P, HH, DH]), ALU.mult)\
                    .then_inc(o_ready, 1)

            def sumsq(n, i):
                s = slice(i * HEADS, (i + 1) * HEADS)
                dve.wait_ge(sq_ready, 2 * n + i + 1)
                wait(dve, rr_ready, 2 * n)
                nc.vector.tensor_reduce(ss[:, s], rot[:, i * INNER:(i + 1) * INNER].rearrange("p (h d) -> p h d", d=DH),
                                        AX.X, ALU.add).then_inc(ss_ready, 1)

            def norm_cos(n, gs, i):
                s = slice(i * HEADS, (i + 1) * HEADS)
                q = raw[:, i * INNER:(i + 1) * INNER].rearrange("p (h d) -> p h d", d=DH)
                dve.wait_ge(rr_ready, 2 * n + i + 1)
                nc.vector.tensor_tensor(q, q, rr[:, s].unsqueeze(2).broadcast_to([P, HEADS, DH]), ALU.mult)\
                    .then_inc(qn_ready, 1)
                dve.wait_ge(qn_ready, 2 * n + i + 1)
                tab = TC[:, bass.ds(layer(n), 1), gs % TPB, i, :]
                nc.vector.tensor_tensor(rot[:, i * INNER:(i + 1) * INNER].rearrange("p (h d) -> p h d", d=DH), q,
                                        tab.broadcast_to([P, HEADS, DH]), ALU.mult).then_inc(cosp_ready, 1)

            def rotated(n, i):
                dve.wait_ge(sinp_ready, 2 * n + i + 1)
                dve.wait_ge(cosp_ready, 2 * n + i + 1)
                r = slice(i * INNER, (i + 1) * INNER)
                nc.vector.tensor_tensor(rot[:, r], rot[:, r], swp[:, r], ALU.add).then_inc(rot_ready, 1)

            def slot(g, gs, do_p, do_a, do_f):
                n, a, u, par = g, g - 1, g - 2, gs % 2
                if do_a:
                    maxes(a, 0)
                if do_f:
                    dve.wait_ge(wo_done, u + 1)
                    dve.wait_ge(y_ready, NT + u)
                    nc.vector.tensor_tensor(xf[:, :].unsqueeze(1), bank[6][:, 0:P].unsqueeze(1),
                                            Y[:, bass.ds(u % NT, 1), :], ALU.add).then_inc(xf_ready, 1)
                if do_a:
                    maxes(a, 1)
                    sums(a, 0)
                if do_p:
                    sumsq(n, 0)
                if do_f:
                    dve.wait_ge(fback_done, u + 1)
                    wait(dve, mv_ready, u)
                    nc.vector.bn_stats(st[:, :], bank[6][:, 0:P]).then_inc(st_ready, 1)
                    dve.wait_ge(st_ready, u + 1)
                    wait(dve, rstd_ready, u)
                    alone(dve)
                    nc.vector.bn_aggr(mv[:, :], st[:, :]).then_inc(mv_ready, 1)
                if do_a:
                    sums(a, 1)
                if do_f:
                    dve.wait_ge(rstd_ready, u + 1)
                    dve.wait_ge(mv_ready, u + 1)
                    wait(dve, xnT_done, u)
                    nc.vector.tensor_scalar(xn[:, :], bank[6][:, 0:P], mv[:, 0:1], rstd[:, 0:1],
                                            ALU.subtract, ALU.mult).then_inc(xn_ready, 1)
                if do_p:
                    norm_cos(n, gs, 0)
                    sumsq(n, 1)
                if do_a:
                    outputs(a, 0)
                if do_p:
                    norm_cos(n, gs, 1)
                if do_a:
                    outputs(a, 1)
                if do_f:
                    dve.wait_ge(ge_ready, u + 1)
                    dve.wait_ge(lin_done, u + 1)
                    wait(dve, w2_done, u)
                    for c, (h0, hn) in enumerate(HC):
                        last = nc.vector.scalar_tensor_tensor(
                            out=hh[0:hn, c, :], in0=bank[6][0:hn, c * P:(c + 1) * P], scalar=b1[0:hn, c:c + 1],
                            in1=ge[0:hn, c, :], op0=ALU.add, op1=ALU.mult)
                    last.then_inc(hh_ready, 1)
                if do_p:
                    rotated(n, 0)
                if do_f:
                    dve.wait_ge(w2_done, u + 1)
                    dve.wait_ge(xp_ready, u + 1)
                    nc.vector.tensor_tensor(Y[:, bass.ds(u % NT, 1), :], bank[6][:, 0:P].unsqueeze(1),
                                            xf[:, :].unsqueeze(1), ALU.add).then_inc(y_ready, 1)
                if do_p:
                    rotated(n, 1)

            slots(dve, slot)

            dve.wait_ge(y_ready, NT + NI)
            dve.wait_ge(a_x1, B)
            for b in range(B):
                yb = Y[:, b * TPB:(b + 1) * TPB, :]
                nc.vector.tensor_tensor(yb, yb, GB[:, b, :].unsqueeze(1).broadcast_to([P, TPB, D]), ALU.mult)\
                    .then_inc(fin_mul, 1)
                wait(dve, fin_mul, b + 1)
                nc.vector.tensor_tensor(yb, yb, X1[:, b * TPB:(b + 1) * TPB, :], ALU.add).then_inc(fin_ready, 1)


def kernel(**inputs):
    import concourse.bacc as bacc
    from concourse.bass_utils import run_bass_kernel_spmd

    f = lambda name: np.asarray(inputs[name])
    tc, ts, mask, eye = tables()
    col = lambda name: f(name).reshape(D, 1)
    arrays = {
        "x": f("L0_attn_x"),
        "wq": f("L0_attn_Wq").T, "wk": f("L0_attn_Wk").T, "wv": f("L0_attn_Wv").T, "wo": f("L0_attn_Wo").T,
        "bq": col("L0_attn_bq"), "bk": col("L0_attn_bk"), "bv": col("L0_attn_bv"), "bo": col("L0_attn_bo"),
        "cT": f("L0_c").T, "wmod": f("L0_wmod").reshape(D, 6, D),
        "wqkv": f("L0_ffn_Wqkv"), "qs": f("L0_ffn_q_scale"), "ks": f("L0_ffn_k_scale"), "fwo": f("L0_ffn_Wo"),
        "ln_g": f("L0_ffn_ln_g").reshape(DEPTH, D, 1), "ln_b": f("L0_ffn_ln_b").reshape(DEPTH, D, 1),
        "w1": f("L0_ffn_W1"), "b1": f("L0_ffn_b1").reshape(DEPTH, 2 * HID, 1),
        "w2": f("L0_ffn_W2"), "b2": f("L0_ffn_b2").reshape(DEPTH, 1, D),
        "tab_cos": tc, "tab_sin": ts, "mask": mask, "eye": eye,
    }
    arrays = {k: np.ascontiguousarray(v) for k, v in arrays.items()}
    nc = bacc.Bacc("TRN2", target_bir_lowering=False, num_devices=1)
    args = [nc.dram_tensor("d_" + k, v.shape, mybir.dt.from_np(v.dtype), kind="ExternalInput").ap()
            for k, v in arrays.items()]
    out = nc.dram_tensor("d_out", (B, S, D), F32, kind="ExternalOutput").ap()
    adaln_block(nc, *args, out)
    r = run_bass_kernel_spmd(nc, [{"d_" + k: v for k, v in arrays.items()}], core_ids=[0])
    return r.results[0]["d_out"]
```

```python
import concourse.bass as bass
from concourse import mybir
from contextlib import ExitStack
import numpy as np

F32 = mybir.dt.float32
BF16 = mybir.dt.bfloat16
ALU = mybir.AluOpType
ACT = mybir.ActivationFunctionType
AX = mybir.AxisListType

B, S, D = 8, 512, 128
DEPTH = 6
HEADS, DH, W = 16, 64, 32
INNER = HEADS * DH
HID = int(D * 4 * 2 / 3)
P = 128
TPB = S // P
NT = B * TPB
NI = DEPTH * NT
NWIN = P // W
HC = [(0, 128), (128, 128), (256, HID - 256)]
NCH = 3 * INNER // 512
HH = HEADS // 2
EPS = 1e-5
MASKED = -1e30


def tables():
    half = np.arange(0, DH, 2, dtype=np.float32)
    inv_freq = (1.0 / 10000.0 ** (half / DH)).astype(np.float32)
    t = np.arange(S, dtype=np.float32)
    freqs = (t[:, None] * inv_freq[None, :]).astype(np.float32)
    freqs = np.concatenate([freqs, freqs], -1).astype(np.float64)
    base = (half + 0.4 * DH) / (1.4 * DH)
    power = (t - S // 2) / (W // 2)
    scale = base[None, :].astype(np.float64) ** power[:, None]
    scale = np.concatenate([scale, scale], -1)
    sign = np.where(np.arange(DH) < DH // 2, -1.0, 1.0)
    cos, sin = np.cos(freqs), np.sin(freqs) * sign
    c = np.stack([cos * scale * 8.0, cos / scale], 1)
    s = np.stack([sin * scale * 8.0, sin / scale], 1)
    c = c.reshape(TPB, P, 2, DH).transpose(1, 0, 2, 3)
    s = s.reshape(TPB, P, 2, DH).transpose(1, 0, 2, 3)
    i = np.arange(P) % W
    w = np.arange(P) // W
    j = np.arange(W)
    prev = np.where(j[None, :] >= i[:, None], 0.0, MASKED)
    own = np.where(j[None, :] <= i[:, None], 0.0, MASKED)
    first = np.where(w[:, None] == 0, MASKED, prev)
    m = np.stack([np.concatenate([prev, own], 1), np.concatenate([first, own], 1)], 1)
    return (np.ascontiguousarray(c, np.float32), np.ascontiguousarray(s, np.float32),
            np.ascontiguousarray(m, np.float32), np.eye(P, dtype=np.float32))


def wait(eng, sem, value):
    if type(value) is int and value <= 0:
        return
    eng.wait_ge(sem, value)


def adaln_block(nc, x_d, wq_d, wk_d, wv_d, wo_d, bq_d, bk_d, bv_d, bo_d, cT_d, wmod_d,
                wqkv_d, qs_d, ks_d, fwo_d, g_d, bln_d, w1_d, b1_d, w2_d, b2_d,
                tc_d, ts_d, mask_d, eye_d, out_d):
    ctx = ExitStack()
    with ctx:
        def sb(name, shape, dt=F32):
            return ctx.enter_context(nc.sbuf_tensor(name, shape, dt))

        def sem(name):
            return ctx.enter_context(nc.semaphore(name))

        X1 = sb("X1", [P, NT, D])
        Y = sb("Y", [P, NT, D])
        GB = sb("GB", [P, B, D])
        ident = sb("ident", [P, P])
        identb = sb("identb", [P, P], BF16)
        maskf = sb("maskf", [P, 2, DH])
        maskb = sb("maskb", [P, 2, HH, DH], BF16)
        TC = sb("TC", [P, DEPTH, TPB, 2, DH])
        TS = sb("TS", [P, DEPTH, TPB, 2, DH])
        qks = sb("qks", [P, DEPTH, 2, DH])
        aw = sb("aw", [P, 4, D])
        ab = sb("ab", [P, 4])
        cT = sb("cT", [P, B])
        sc = sb("sc", [P, 2, B])
        wmod = sb("wmod", [P, 6, D])
        modT = sb("modT", [P, 6, B])
        gt = sb("gt", [P, 2, B])
        cur = sb("cur", [P, 6])
        wqkv = sb("wqkv", [P, NCH, 512])
        fwo = sb("fwo", [P, INNER // P, D])
        w1 = sb("w1", [P, 2 * HID])
        w2 = sb("w2", [P, 3, D])
        fv = sb("fv", [P, 2])
        b1 = sb("b1", [P, 6])
        b2 = sb("b2", [1, D])
        ones = sb("ones", [1, P])
        nhalf = sb("nhalf", [P, 2 * HEADS])
        xp = sb("xp", [P, 2, D])
        xs = sb("xs", [P, 2, P + 1])
        raw = sb("raw", [P, 2 * INNER])
        rot = sb("rot", [P, 2 * INNER])
        swp = sb("swp", [P, 2 * INNER])
        ss = sb("ss", [P, 2 * HEADS])
        ssm = sb("ssm", [P, 2 * HEADS])
        rr = sb("rr", [P, 2 * HEADS])
        qT = sb("qT", [P, 2, HH, P])
        kT = sb("kT", [P, 2, HH, W + P])
        V = sb("V", [P, 2, INNER])
        Vp = sb("Vp", [P, 2, INNER])
        mx = sb("mx", [P, 2, HH])
        Pr = sb("Pr", [P, 2, 512])
        PB = sb("PB", [P, 2, HH, P])
        PT = sb("PT", [P, 2, HH, P])
        BT = sb("BT", [P, 2, HH, W])
        sm = sb("sm", [P, 2, HH])
        rs = sb("rs", [P, 2, HH])
        OT = sb("OT", [P, INNER // P, P])
        xf = sb("xf", [P, D])
        fs = sb("fs", [P, 2, P + 1])
        st = sb("st", [P, 6])
        mv = sb("mv", [P, 2])
        vpe = sb("vpe", [P, 1])
        rstd = sb("rstd", [P, 1])
        xn = sb("xn", [P, D])
        xnT = sb("xnT", [P, P])
        ge = sb("ge", [P, 3, P])
        hh = sb("hh", [P, 3, P])
        ax = raw[:, 0:512].rearrange("p (j f) -> p j f", j=TPB)
        an = raw[:, 512:1024].rearrange("p (j f) -> p j f", j=TPB)
        ah = raw[:, 1024:1536]
        a2 = raw[:, 1536:2048].rearrange("p (j f) -> p j f", j=TPB)
        aq = rot[:, 0:512]
        ak = rot[:, 512:1024]
        av = rot[:, 1024:1536].rearrange("p (j f) -> p j f", j=TPB)
        ao = rot[:, 1536:2048]
        apT = swp[:, :].rearrange("p (t s) -> p t s", t=TPB)
        ath = [qT[:, i, 0:4, :].rearrange("p a b -> p (a b)") for i in range(2)]
        ath2 = [qT[:, i, 4:8, :].rearrange("p a b -> p (a b)") for i in range(2)]
        are = [Pr[:, i, :] for i in range(2)]
        tcb = sb("tcb", [P, TPB, 2, DH])
        tsb = sb("tsb", [P, TPB, 2, DH])
        ast = sb("ast", [P, TPB, 6])
        amv = sb("amv", [P, TPB, 2])
        ave = sb("ave", [P, TPB])
        ars = sb("ars", [P, TPB])
        anm = sb("anm", [P, TPB])
        asum = sb("asum", [P, TPB])
        arc = sb("arc", [P, TPB])
        ay = PT[:, 0, 0:4, :].rearrange("p a b -> p (a b)")
        ah2 = PT[:, 1, 0:4, :].rearrange("p a b -> p (a b)")

        bank = [ctx.enter_context(nc.psum_tensor(f"bank{i}", [P, 512], F32)) for i in range(8)]

        QK_BANK = (2, 5, 2, 5)
        PT_BANK = (3, 4, 3, 4)

        ld_const = sem("ld_const")
        ld_attn = sem("ld_attn")
        ld_x = sem("ld_x")
        wq_loaded = [sem(f"wq_loaded{c}") for c in range(NCH)]
        fw_loaded = sem("fw_loaded")
        vp_moved = sem("vp_moved")
        out_stored = sem("out_stored")
        passed = sem("passed")
        silu_in = sem("silu_in")
        silu_mul = sem("silu_mul")
        mod_done = sem("mod_done")
        mod_ready = sem("mod_ready")
        ones_ready = sem("ones_ready")
        mask_ready = sem("mask_ready")
        silu_add = sem("silu_add")
        zero_ready = sem("zero_ready")
        a_stats = sem("a_stats")
        a_aggr = sem("a_aggr")
        a_var = sem("a_var")
        a_rstd = sem("a_rstd")
        a_norm = sem("a_norm")
        a_nT = sem("a_nT")
        a_cur = sem("a_cur")
        a_h = sem("a_h")
        a_proj = sem("a_proj")
        a_qs = sem("a_qs")
        a_ks = sem("a_ks")
        a_vs = sem("a_vs")
        a_score = sem("a_score")
        a_act = sem("a_act")
        a_theta1 = sem("a_theta1")
        a_theta = sem("a_theta")
        a_max = sem("a_max")
        a_exp = sem("a_exp")
        a_recip = sem("a_recip")
        a_prob = sem("a_prob")
        a_pT = sem("a_pT")
        a_pTs = sem("a_pTs")
        a_out = sem("a_out")
        a_outs = sem("a_outs")
        a_y = sem("a_y")
        a_ys = sem("a_ys")
        a_yT = sem("a_yT")
        a_x2 = sem("a_x2")
        a_x1 = sem("a_x1")
        a_back = sem("a_back")
        a_gb = sem("a_gb")
        y_ready = sem("y_ready")
        xp_ready = sem("xp_ready")
        xT_done = sem("xT_done")
        xs_ready = sem("xs_ready")
        xcol_ready = sem("xcol_ready")
        proj_done = sem("proj_done")
        proj_out = sem("proj_out")
        sq_ready = sem("sq_ready")
        ss_ready = sem("ss_ready")
        ssm_ready = sem("ssm_ready")
        rr_ready = sem("rr_ready")
        qn_ready = sem("qn_ready")
        cosp_ready = sem("cosp_ready")
        sinp_ready = sem("sinp_ready")
        rot_ready = sem("rot_ready")
        qkT_done = sem("qkT_done")
        qkT_out = sem("qkT_out")
        kprev_ready = sem("kprev_ready")
        score_done = sem("score_done")
        max_ready = sem("max_ready")
        sub_ready = sem("sub_ready")
        exp_ready = sem("exp_ready")
        sum_ready = sem("sum_ready")
        rsum_ready = sem("rsum_ready")
        prob_ready = sem("prob_ready")
        prev_ready = sem("prev_ready")
        band_ready = sem("band_ready")
        pT_done = sem("pT_done")
        pT_out = sem("pT_out")
        pv_done = sem("pv_done")
        oT_out = sem("oT_out")
        wo_done = sem("wo_done")
        xf_ready = sem("xf_ready")
        fT_done = sem("fT_done")
        fs_ready = sem("fs_ready")
        fcol_ready = sem("fcol_ready")
        fback_done = sem("fback_done")
        st_ready = sem("st_ready")
        mv_ready = sem("mv_ready")
        vpe_ready = sem("vpe_ready")
        rstd_ready = sem("rstd_ready")
        xn_ready = sem("xn_ready")
        xnT_done = sem("xnT_done")
        xnT_ready = sem("xnT_ready")
        gate_done = sem("gate_done")
        lin_done = sem("lin_done")
        ge_ready = sem("ge_ready")
        hh_ready = sem("hh_ready")
        w2_done = sem("w2_done")
        fin_mul = sem("fin_mul")
        fin_ready = sem("fin_ready")

        LAG = 2
        GROUPS = NI // TPB - 1

        def slots(eng, body):
            for g in range(TPB + LAG):
                body(g, g)
            with eng.Fori(1, GROUPS) as k:
                for i in range(TPB):
                    body(k * TPB + (LAG + i), LAG + i)
            for g in range(TPB * GROUPS + LAG, NI + LAG):
                body(g, g)

        def step(g, gs, lag, do, *part):
            if type(g) is not int or 0 <= g - lag < NI:
                do(g - lag, (gs - lag) % TPB, *part)

        def batches(eng, body):
            body(0)
            with eng.Fori(1, B) as b:
                body(b)

        block = ctx.enter_context(nc.Block())
        FWL = 13 * 16
        CONST = (4 + 2 * DEPTH) * 16

        def layer(n):
            return n // NT

        def alone(eng):
            eng.sem_inc(passed, 1)

        @block.sync
        def _(sp):
            for dst, src in ((ident[:, :], eye_d), (maskf[:, :, :], mask_d),
                             (tcb[:, :, :, :], tc_d), (tsb[:, :, :, :], ts_d)):
                sp.dma_start(dst, src).then_inc(ld_const, 16)
            for l in range(DEPTH):
                for i, s_d in enumerate((qs_d, ks_d)):
                    sp.dma_start(qks[:, l, i, :], s_d[l:l + 1, :].broadcast_to([P, DH])).then_inc(ld_const, 16)
            for i, w_d in enumerate((wq_d, wk_d, wv_d, wo_d)):
                sp.dma_start(aw[:, i, :], w_d).then_inc(ld_attn, 16)
            for i, b_d in enumerate((bq_d, bk_d, bv_d, bo_d)):
                sp.dma_start(ab[:, i:i + 1], b_d).then_inc(ld_attn, 16)
            sp.dma_start(cT[:, :], cT_d).then_inc(ld_attn, 16)
            sp.dma_start(wmod[:, :, :], wmod_d).then_inc(ld_attn, 16)
            for b in range(B):
                wait(sp, a_x2, b)
                wait(sp, a_yT, b)
                sp.dma_start(ax, x_d[b].rearrange("(j p) f -> p j f", p=P)).then_inc(ld_x, 16)

            def shift_v(n, par):
                if type(n) is int and n == 0:
                    sp.wait_ge(zero_ready, 1)
                else:
                    sp.wait_ge(proj_out, n * NCH)
                    alone(sp)
                wait(sp, pv_done, n * 2 - 2)
                alone(sp)
                wait(sp, vp_moved, n * 16)
                alone(sp)
                sp.dma_start(Vp[0:W, par, :], V[P - W:P, 1 - par, :]).then_inc(vp_moved, 16)

            def loads_and_moves(l):
                for c in range(NCH):
                    wait(sp, proj_done, l * (NT * NCH) + (c + 1 - NCH))
                    alone(sp)
                    sp.dma_start(wqkv[:, c, :], wqkv_d[l, :, c * 512:(c + 1) * 512]).then_inc(wq_loaded[c], 16)
                for j in range(2):
                    shift_v(l * NT + j, j % 2)
                wait(sp, w2_done, l * NT)
                alone(sp)
                sp.dma_start(fwo[:, :, :], fwo_d[l].rearrange("(c p) n -> p c n", p=P)).then_inc(fw_loaded, 16)
                sp.dma_start(w1[:, :], w1_d[l]).then_inc(fw_loaded, 16)
                sp.dma_start(w2[:, 0:2, :], w2_d[l, 0:256, :].rearrange("(c p) n -> p c n", p=P)).then_inc(fw_loaded, 16)
                sp.dma_start(w2[0:HID - 256, 2, :], w2_d[l, 256:HID, :]).then_inc(fw_loaded, 16)
                sp.dma_start(fv[:, 0:1], g_d[l]).then_inc(fw_loaded, 16)
                sp.dma_start(fv[:, 1:2], bln_d[l]).then_inc(fw_loaded, 16)
                for i in range(2):
                    for c, (h0, hn) in enumerate(HC):
                        sp.dma_start(b1[0:hn, 3 * i + c:3 * i + c + 1],
                                     b1_d[l, i * HID + h0:i * HID + h0 + hn, :]).then_inc(fw_loaded, 16)
                sp.dma_start(b2[:, :], b2_d[l]).then_inc(fw_loaded, 16)
                for j in range(2, TPB):
                    shift_v(l * NT + j, j % 2)
                with sp.Fori(1, B) as b:
                    for j in range(TPB):
                        shift_v(l * NT + b * TPB + j, j % 2)

            loads_and_moves(0)
            with sp.Fori(1, DEPTH) as l:
                loads_and_moves(l)
            for b in range(B):
                sp.wait_ge(fin_ready, b + 1)
                sp.dma_start(out_d[b].rearrange("(j p) f -> p j f", p=P),
                             Y[:, b * TPB:(b + 1) * TPB, :]).then_inc(out_stored, 16)
            sp.wait_ge(out_stored, 16 * B)

        @block.tensor
        def _(pe):
            pe.wait_ge(ld_attn, 160)
            pe.wait_ge(silu_mul, 1)
            for i in range(6):
                mm = nc.tensor.matmul(bank[0][:, i * B:(i + 1) * B], wmod[:, i, :], sc[:, 1, :], start=True, stop=True)
            mm.then_inc(mod_done, 1)
            pe.wait_ge(ld_const, CONST)
            pe.wait_ge(mod_ready, 1)

            def first_attention(b):
                wait(pe, a_norm, 2 * b + 1)
                wait(pe, a_outs, b)
                wait(pe, a_h, 2 * b)
                for j in range(TPB):
                    mm = nc.tensor.transpose(bank[0][:, j * P:(j + 1) * P], an[:, j, :], ident[:, :])
                mm.then_inc(a_nT, 1)
                wait(pe, a_h, 2 * b + 1)
                wait(pe, y_ready, TPB * b)
                wait(pe, a_gb, b)
                nc.tensor.matmul(bank[1][:, :], aw[:, 0, :], ah, start=True, stop=True).then_inc(a_proj, 1)
                nc.tensor.matmul(bank[2][:, :], aw[:, 1, :], ah, start=True, stop=True).then_inc(a_proj, 1)
                for j in range(TPB):
                    mm = nc.tensor.matmul(bank[3][:, j * P:(j + 1) * P], ah[:, j * P:(j + 1) * P], aw[:, 2, :],
                                          start=True, stop=True)
                mm.then_inc(a_proj, 1)
                wait(pe, a_qs, b + 1)
                wait(pe, a_ks, b + 1)
                for j in range(TPB):
                    nc.tensor.matmul(bank[4 + j][:, :], aq[:, j * P:(j + 1) * P], ak, start=True, stop=True)\
                        .then_inc(a_score, 1)
                for j in range(TPB):
                    wait(pe, a_prob, TPB * b + j + 1)
                    for u in range(TPB):
                        mm = nc.tensor.transpose(bank[4 + j][:, u * P:(u + 1) * P], are[j % 2][:, u * P:(u + 1) * P],
                                                 ident[:, :])
                    mm.then_inc(a_pT, 1)
                wait(pe, a_pTs, TPB * (b + 1))
                wait(pe, a_vs, b + 1)
                for u in range(TPB):
                    mm = nc.tensor.matmul(bank[0][:, :], av[:, u, :], apT[:, u, :], start=(u == 0), stop=(u == TPB - 1))
                mm.then_inc(a_out, 1)
                wait(pe, a_outs, b + 1)
                nc.tensor.matmul(bank[1][:, :], aw[:, 3, :], ao, start=True, stop=True).then_inc(a_y, 1)
                wait(pe, a_ys, b + 1)
                for j in range(TPB):
                    mm = nc.tensor.transpose(bank[2][:, j * P:(j + 1) * P], ay[:, j * P:(j + 1) * P], ident[:, :])
                mm.then_inc(a_yT, 1)
                wait(pe, a_norm, 2 * b + 2)
                for j in range(TPB):
                    mm = nc.tensor.transpose(bank[0][:, j * P:(j + 1) * P], an[:, j, :], ident[:, :])
                mm.then_inc(a_nT, 1)
                nc.tensor.matmul(bank[3][:, 0:P], cur[:, 5:6].broadcast_to([P, P]), ident[:, :], start=True, stop=True)
                wait(pe, a_h, 2 * b + 2)
                for j in range(TPB):
                    mm = nc.tensor.transpose(bank[1][:, j * P:(j + 1) * P], ah2[:, j * P:(j + 1) * P], ident[:, :])
                mm.then_inc(a_back, 1)

            batches(pe, first_attention)

            def x_back(n, j):
                pe.wait_ge(xp_ready, n + 1)
                wait(pe, qkT_out, 4 * n - 1)
                nc.tensor.transpose(bank[2][:, 0:P], xp[:, j % 2, :], ident[:, :]).then_inc(xT_done, 1)

            def proj(n, j, c):
                if c == 0:
                    pe.wait_ge(xs_ready, n + 1)
                    pe.wait_ge(xcol_ready, n + 1)
                wait(pe, proj_out, n * NCH + (c - 1))
                if c < 2:
                    wait(pe, oT_out, 2 * n - 3 + c)
                pe.wait_ge(wq_loaded[c], layer(n) * 16 + 16)
                nc.tensor.matmul(bank[c % 2][:, :], xs[:, j % 2, 0:P], wqkv[:, c, :], start=True, stop=True)\
                    .then_inc(proj_done, 1)

            def qk_back(n, j, i):
                pe.wait_ge(rot_ready, 2 * n + i // 2 + 1)
                if i == 0:
                    pe.wait_ge(xs_ready, n + 1)
                else:
                    wait(pe, qkT_out, 4 * n - (0 if i == 1 else 1 - i))
                for u in range(4):
                    col = (4 * i + u) * P
                    mm = nc.tensor.transpose(bank[QK_BANK[i]][:, u * P:(u + 1) * P], rot[:, col:col + P], ident[:, :])
                mm.then_inc(qkT_done, 1)

            def scores(a, j, h):
                if h == 0:
                    pe.wait_ge(qkT_out, 4 * a + 4)
                    pe.wait_ge(kprev_ready, a + 1)
                wait(pe, pT_out, 4 * a - 1 + h)
                nc.tensor.matmul(bank[3 + h][:, :], identb[:, :],
                                 maskb[:, 1 if j == 0 else 0, :, :].rearrange("p h k -> p (h k)"),
                                 start=True, stop=False, skip_group_check=True)
                r = slice(h * DH, (h + 1) * DH)
                for w in range(NWIN):
                    for u in range(HH):
                        mm = nc.tensor.matmul(bank[3 + h][w * W:(w + 1) * W, u * DH:(u + 1) * DH],
                                              qT[r, j % 2, u, w * W:(w + 1) * W],
                                              kT[r, j % 2, u, w * W:w * W + 2 * W],
                                              start=False, stop=True, skip_group_check=True)
                mm.then_inc(score_done, 1)

            def probs_back(a, j, i):
                h = i // 2
                pe.wait_ge(band_ready, 2 * a + h + 1)
                if i == 1:
                    pe.wait_ge(sub_ready, 2 * a + 2)
                if i >= 2:
                    pe.wait_ge(pT_out, 4 * a + i - 1)
                for u in range(4):
                    mm = nc.tensor.transpose(bank[PT_BANK[i]][:, u * P:(u + 1) * P],
                                             PB[:, h, 4 * (i % 2) + u, :], ident[:, :])
                mm.then_inc(pT_done, 1)

            def pv(a, j, h):
                pe.wait_ge(pT_out, 4 * a + 2 * h + 2)
                pe.wait_ge(prev_ready, 2 * a + h + 1)
                pe.wait_ge(vp_moved, 16 * a + 16)
                ahead = min(a + 2, NI) if type(a) is int else a + 2
                pe.wait_ge(proj_out, NCH * ahead)
                for u in range(HH):
                    hc = (2 * u + h) * DH
                    dst = bank[u // 4][h * DH:(h + 1) * DH, (u % 4) * P:(u % 4 + 1) * P]
                    nc.tensor.matmul(dst, V[:, j % 2, hc:hc + DH], PT[:, h, u, :], start=True, stop=False,
                                     skip_group_check=True)
                    mm = nc.tensor.matmul(dst[:, 0:W], Vp[:, j % 2, hc:hc + DH], BT[:, h, u, :], start=False,
                                          stop=True, skip_group_check=True)
                mm.then_inc(pv_done, 1)

            def out_proj(u, j):
                pe.wait_ge(oT_out, 2 * u + 2)
                pe.wait_ge(y_ready, NT + u)
                pe.wait_ge(fw_loaded, layer(u) * FWL + FWL)
                for c in range(INNER // P):
                    mm = nc.tensor.matmul(bank[6][:, 0:P], OT[:, c, :], fwo[:, c, :],
                                          start=(c == 0), stop=(c == INNER // P - 1))
                mm.then_inc(wo_done, 1)

            def ffn_x_back(u, j):
                pe.wait_ge(xf_ready, u + 1)
                nc.tensor.transpose(bank[7][:, 0:P], xf[:, :], ident[:, :]).then_inc(fT_done, 1)

            def ffn_x_forth(u, j):
                pe.wait_ge(fs_ready, u + 1)
                pe.wait_ge(fcol_ready, u + 1)
                nc.tensor.transpose(bank[6][:, 0:P], fs[:, j % 2, 0:P], ident[:, :]).then_inc(fback_done, 1)

            def ffn_norm_back(u, j):
                pe.wait_ge(xn_ready, u + 1)
                nc.tensor.transpose(bank[7][:, 0:P], xn[:, :], ident[:, :]).then_inc(xnT_done, 1)

            def ffn_in(u, j, i):
                pe.wait_ge(xnT_ready, u + 1)
                bk, done = ((bank[6], lin_done), (bank[7], gate_done))[i]
                for c, (h0, hn) in enumerate(HC):
                    mm = nc.tensor.matmul(bk[0:hn, c * P:(c + 1) * P], w1[:, i * HID + h0:i * HID + h0 + hn],
                                          xnT[:, :], start=True, stop=True)
                mm.then_inc(done, 1)

            def ffn_out(u, j):
                pe.wait_ge(hh_ready, u + 1)
                for c, (h0, hn) in enumerate(HC):
                    nc.tensor.matmul(bank[6][:, 0:P], hh[0:hn, c, :], w2[0:hn, c, :], start=(c == 0), stop=False)
                nc.tensor.matmul(bank[6][:, 0:P], ones[:, :], b2[:, :], start=False, stop=True).then_inc(w2_done, 1)

            def slot(g, gs):
                step(g, gs, 0, x_back)
                step(g, gs, 2, ffn_x_forth)
                step(g, gs, 0, proj, 0)
                step(g, gs, 0, proj, 1)
                step(g, gs, 0, proj, 2)
                step(g, gs, 0, proj, 3)
                step(g, gs, 1, scores, 1)
                step(g, gs, 2, ffn_norm_back)
                step(g, gs, 0, proj, 4)
                step(g, gs, 0, proj, 5)
                step(g, gs, 1, probs_back, 0)
                step(g, gs, 1, probs_back, 1)
                step(g, gs, 2, ffn_in, 1)
                step(g, gs, 2, ffn_in, 0)
                step(g, gs, 1, pv, 0)
                step(g, gs, 2, ffn_out)
                step(g, gs, 1, probs_back, 2)
                step(g, gs, 1, probs_back, 3)
                step(g, gs, 0, qk_back, 0)
                step(g, gs, 0, qk_back, 1)
                step(g, gs, 1, pv, 1)
                step(g, gs, 0, qk_back, 2)
                step(g, gs, 0, qk_back, 3)
                step(g, gs, 1, out_proj)
                step(g, gs, 0, scores, 0)
                step(g, gs, 1, ffn_x_back)

            pe.wait_ge(ones_ready, 1)
            pe.wait_ge(mask_ready, 1)
            pe.wait_ge(a_gb, B)
            slots(pe, slot)

        @block.scalar
        def _(act):
            act.wait_ge(ld_attn, 160)
            nc.scalar.activation(sc[:, 0, :], cT[:, :], ACT.Tanh, scale=0.5).then_inc(silu_in, 1)

            def theta_parts(b, j):
                wait(act, a_score, TPB * b + j + 1)
                wait(act, a_theta, TPB * b + j - 1 if j >= 2 else TPB * b)
                wait(act, a_pT, TPB * b + j - 1 if j >= 2 else TPB * b)
                nc.scalar.activation(ath[j % 2], bank[4 + j][:, :], ACT.Tanh, scale=0.5)
                nc.scalar.activation(ath2[j % 2], bank[4 + j][:, :], ACT.Tanh)
                nc.scalar.activation(are[j % 2], bank[4 + j][:, :], ACT.Relu, scale=0.1).then_inc(a_act, 1)

            def exps(b, j):
                wait(act, a_max, TPB * b + j + 1)
                nc.scalar.activation(are[j % 2], are[j % 2], ACT.Exp, bias=anm[:, j:j + 1],
                                     accum_out=asum[:, j:j + 1]).then_inc(a_exp, 1)

            def probs_out(b, j):
                wait(act, a_pT, TPB * b + j + 1)
                nc.scalar.activation(apT[:, :, j * P:(j + 1) * P],
                                     bank[4 + j][:, :].rearrange("p (u s) -> p u s", u=TPB), ACT.Copy)\
                    .then_inc(a_pTs, 1)

            def first_attention(b):
                wait(act, a_nT, 2 * b + 1)
                wait(act, a_cur, b + 1)
                wait(act, a_proj, 3 * b)
                nc.scalar.activation(ah, bank[0][:, :], ACT.Identity, scale=cur[:, 1:2], bias=cur[:, 0:1]).then_inc(a_h, 1)
                wait(act, a_proj, 3 * b + 2)
                nc.scalar.activation(ak, bank[2][:, :], ACT.Identity, bias=ab[:, 1:2], scale=1.0).then_inc(a_ks, 1)
                wait(act, a_out, b)
                theta_parts(b, 0)
                theta_parts(b, 1)
                exps(b, 0)
                exps(b, 1)
                probs_out(b, 0)
                theta_parts(b, 2)
                probs_out(b, 1)
                theta_parts(b, 3)
                exps(b, 2)
                exps(b, 3)
                probs_out(b, 2)
                probs_out(b, 3)
                wait(act, a_nT, 2 * b + 2)
                wait(act, a_back, b)
                nc.scalar.activation(ah2, bank[0][:, :], ACT.Identity, scale=cur[:, 4:5], bias=cur[:, 3:4]).then_inc(a_h, 1)

            batches(act, first_attention)

            def shifted(n, j):
                act.wait_ge(xT_done, n + 1)
                wait(act, xcol_ready, n)
                nc.scalar.activation(xs[0:64, j % 2, 0:P], bank[2][0:64, 0:P], ACT.Copy)
                nc.scalar.activation(xs[64:P, j % 2, 1:P + 1], bank[2][64:P, 0:P], ACT.Copy).then_inc(xs_ready, 1)

            def to_raw(n, j, c):
                act.wait_ge(proj_done, NCH * n + c + 1)
                if c % 2 == 0:
                    wait(act, sinp_ready, 2 * n - 1 + c // 2)
                    wait(act, cosp_ready, 2 * n - 1 + c // 2)
                nc.scalar.activation(raw[:, c * 512:(c + 1) * 512], bank[c % 2][:, :], ACT.Copy).then_inc(proj_out, 1)

            def squares(n, j, i):
                act.wait_ge(proj_out, NCH * n + 2 * i + 2)
                wait(act, qkT_done, 4 * n - 2 + 2 * i)
                nc.scalar.activation(rot[:, i * INNER:(i + 1) * INNER], raw[:, i * INNER:(i + 1) * INNER],
                                     ACT.Square).then_inc(sq_ready, 1)

            def to_v(n, j, c):
                act.wait_ge(proj_done, NCH * n + c + 1)
                if c == 4:
                    wait(act, pv_done, 2 * n - 2)
                    wait(act, vp_moved, 16 * n)
                nc.scalar.activation(V[:, j % 2, (c - 4) * 512:(c - 3) * 512], bank[c % 2][:, :], ACT.Copy)\
                    .then_inc(proj_out, 1)

            def qk_to_sbuf(n, j, i):
                act.wait_ge(qkT_done, 4 * n + i + 1)
                wait(act, score_done, 2 * n - 2)
                if i < 2:
                    dst = qT[:, j % 2, 4 * i:4 * i + 4, :]
                else:
                    wait(act, kprev_ready, n)
                    dst = kT[:, j % 2, 4 * i - 8:4 * i - 4, W:W + P]
                nc.scalar.activation(dst, bank[QK_BANK[i]][:, :].rearrange("p (c s) -> p c s", c=4), ACT.Copy)\
                    .then_inc(qkT_out, 1)

            def exp_half(a, j, h):
                act.wait_ge(sub_ready, 2 * a + h + 1)
                nc.scalar.activation(Pr[:, h, :], Pr[:, h, :], ACT.Exp).then_inc(exp_ready, 1)

            def to_band(a, j, h):
                act.wait_ge(prob_ready, 2 * a + h + 1)
                wait(act, pT_done, 4 * a - 2 + 2 * h)
                src = Pr[:, h, :].rearrange("p (u k) -> p u k", u=HH)
                nc.scalar.activation(PB[0:W, h, :, 0:W], src[0:W, :, W:2 * W], ACT.Copy)
                for w in range(1, NWIN):
                    r = slice(w * W, (w + 1) * W)
                    last = nc.scalar.activation(PB[r, h, :, (w - 1) * W:(w + 1) * W], src[r, :, :], ACT.Copy)
                last.then_inc(band_ready, 1)

            def probs_to_sbuf(a, j, i):
                act.wait_ge(pT_done, 4 * a + i + 1)
                wait(act, pv_done, 2 * a - 1 + i // 2)
                nc.scalar.activation(PT[:, i // 2, 4 * (i % 2):4 * (i % 2) + 4, :],
                                     bank[PT_BANK[i]][:, :].rearrange("p (c s) -> p c s", c=4), ACT.Copy)\
                    .then_inc(pT_out, 1)

            def o_to_sbuf(a, j, i):
                act.wait_ge(pv_done, 2 * a + 2)
                wait(act, wo_done, a)
                nc.scalar.activation(OT[:, 4 * i:4 * i + 4, :], bank[i][:, :].rearrange("p (c s) -> p c s", c=4),
                                     ACT.Copy).then_inc(oT_out, 1)

            def ffn_shifted(u, j):
                act.wait_ge(fT_done, u + 1)
                wait(act, fcol_ready, u)
                nc.scalar.activation(fs[0:64, j % 2, 0:P], bank[7][0:64, 0:P], ACT.Copy)
                nc.scalar.activation(fs[64:P, j % 2, 1:P + 1], bank[7][64:P, 0:P], ACT.Copy).then_inc(fs_ready, 1)

            def ffn_affine(u, j):
                act.wait_ge(xnT_done, u + 1)
                nc.scalar.activation(xnT[:, :], bank[7][:, 0:P], ACT.Identity, scale=fv[:, 0:1], bias=fv[:, 1:2])\
                    .then_inc(xnT_ready, 1)

            def gelu(u, j):
                act.wait_ge(gate_done, u + 1)
                wait(act, hh_ready, u)
                for c, (h0, hn) in enumerate(HC):
                    last = nc.scalar.activation(ge[0:hn, c, :], bank[7][0:hn, c * P:(c + 1) * P], ACT.Gelu,
                                                bias=b1[0:hn, 3 + c:4 + c], scale=1.0)
                last.then_inc(ge_ready, 1)

            def slot(g, gs):
                step(g, gs, 2, o_to_sbuf, 0)
                step(g, gs, 2, o_to_sbuf, 1)
                step(g, gs, 1, qk_to_sbuf, 2)
                step(g, gs, 1, qk_to_sbuf, 3)
                step(g, gs, 2, ffn_shifted)
                step(g, gs, 0, shifted)
                step(g, gs, 1, exp_half, 0)
                step(g, gs, 0, to_raw, 0)
                step(g, gs, 0, to_raw, 1)
                step(g, gs, 0, squares, 0)
                step(g, gs, 0, to_raw, 2)
                step(g, gs, 0, to_raw, 3)
                step(g, gs, 0, squares, 1)
                step(g, gs, 1, to_band, 0)
                step(g, gs, 1, exp_half, 1)
                step(g, gs, 2, ffn_affine)
                step(g, gs, 0, to_v, 4)
                step(g, gs, 0, to_v, 5)
                step(g, gs, 1, probs_to_sbuf, 0)
                step(g, gs, 1, probs_to_sbuf, 1)
                step(g, gs, 2, gelu)
                step(g, gs, 1, to_band, 1)
                step(g, gs, 1, probs_to_sbuf, 2)
                step(g, gs, 1, probs_to_sbuf, 3)
                step(g, gs, 0, qk_to_sbuf, 0)
                step(g, gs, 0, qk_to_sbuf, 1)

            slots(act, slot)

        @block.gpsimd
        def _(pool):
            pool.memset(ones[:, :], 1.0)
            pool.memset(nhalf[:, :], -0.5).then_inc(ones_ready, 1)
            pool.memset(kT[:, :, :, :], 0.0)
            pool.memset(PB[:, :, :, :], 0.0)
            pool.memset(BT[:, :, :, :], 0.0)
            pool.memset(Vp[:, :, :], 0.0)
            pool.memset(V[:, :, :], 0.0).then_inc(zero_ready, 1)
            pool.wait_ge(ones_ready, 1)
            pool.wait_ge(ld_const, CONST)
            for l in range(DEPTH):
                for j in range(TPB):
                    pool.tensor_tensor(TC[:, l, j, :, :], tcb[:, j, :, :], qks[:, l, :, :], ALU.mult)
                    pool.tensor_tensor(TS[:, l, j, :, 0:32], tsb[:, j, :, 0:32], qks[:, l, :, 32:64], ALU.mult)
                    pool.tensor_tensor(TS[:, l, j, :, 32:64], tsb[:, j, :, 32:64], qks[:, l, :, 0:32], ALU.mult)\
                        .then_inc(zero_ready, 1)

            pool.wait_ge(mod_ready, 1)

            def first_attention(b):
                def rstd4(i):
                    wait(pool, a_aggr, 2 * b + i + 1)
                    wait(pool, a_norm, 2 * b + i)
                    alone(pool)
                    pool.tensor_scalar(ave[:, :], amv[:, :, 1], EPS, None, ALU.add).then_inc(a_var, 1)
                    wait(pool, a_var, 2 * b + i + 1)
                    pool.tensor_tensor(ars[:, :], ave[:, :], nhalf[:, 0:TPB], ALU.pow).then_inc(a_rstd, 1)
                wait(pool, a_back, b)
                wait(pool, a_ys, b)
                wait(pool, a_h, 2 * b)
                alone(pool)
                pool.tensor_copy(cur[:, :].unsqueeze(2), modT[:, :, bass.ds(b, 1)]).then_inc(a_cur, 1)
                rstd4(0)
                wait(pool, a_x2, b + 1)
                alone(pool)
                pool.tensor_copy(X1[:, bass.ds(b * TPB, TPB), :], a2).then_inc(a_x1, 1)
                rstd4(1)

            batches(pool, first_attention)

            def take_x(n, j):
                pool.wait_ge(y_ready, n + 1)
                wait(pool, xT_done, n - 1)
                alone(pool)
                pool.tensor_copy(xp[:, j % 2, :].unsqueeze(1), Y[:, bass.ds(n % NT, 1), :]).then_inc(xp_ready, 1)

            def carried(n, j):
                wait(pool, proj_done, NCH * (n - 1))
                wait(pool, xs_ready, n)
                pool.wait_ge(xp_ready, n + 1)
                alone(pool)
                if j == 0:
                    pool.memset(xs[64:P, 0, 0:1], 0.0).then_inc(xcol_ready, 1)
                else:
                    pool.tensor_copy(xs[64:P, j % 2, 0:1], xs[64:P, 1 - j % 2, P:P + 1]).then_inc(xcol_ready, 1)
                pool.wait_ge(xcol_ready, n + 1)

            def ffn_carried(u, j):
                wait(pool, fback_done, u - 1)
                wait(pool, fs_ready, u)
                if type(u) is int and u == NI - 1:
                    pool.wait_ge(kprev_ready, NI)
                    pool.wait_ge(sinp_ready, 2 * NI)
                alone(pool)
                if j == 0:
                    pool.memset(fs[64:P, 0, 0:1], 0.0).then_inc(fcol_ready, 1)
                else:
                    pool.tensor_copy(fs[64:P, j % 2, 0:1], fs[64:P, 1 - j % 2, P:P + 1]).then_inc(fcol_ready, 1)
                pool.wait_ge(fcol_ready, u + 1)

            def norms(n, j, i):
                s = slice(i * HEADS, (i + 1) * HEADS)
                pool.wait_ge(ss_ready, 2 * n + i + 1)
                wait(pool, qn_ready, 2 * n - 1 + i)
                alone(pool)
                pool.tensor_scalar(ssm[:, s], ss[:, s], 1e-24, None, ALU.max).then_inc(ssm_ready, 1)
                pool.wait_ge(ssm_ready, 2 * n + i + 1)
                pool.tensor_tensor(rr[:, s], ssm[:, s], nhalf[:, s], ALU.pow).then_inc(rr_ready, 1)

            def sin_part(n, j, i):
                pool.wait_ge(qn_ready, 2 * n + i + 1)
                wait(pool, rot_ready, 2 * n - 1 + i)
                src = raw[:, i * INNER:(i + 1) * INNER].rearrange("p (h t d) -> p h t d", t=2, d=32)
                dst = swp[:, i * INNER:(i + 1) * INNER].rearrange("p (h t d) -> p h t d", t=2, d=32)
                for t in range(2):
                    tab = TS[:, bass.ds(layer(n), 1), j, i, 32 * t:32 * t + 32]
                    last = pool.tensor_tensor(dst[:, :, t, :], src[:, :, 1 - t, :],
                                              tab.broadcast_to([P, HEADS, 32]), ALU.mult)
                last.then_inc(sinp_ready, 1)

            def keys_before(n, j):
                wait(pool, qkT_out, 4 * n)
                wait(pool, score_done, 2 * n - 2)
                alone(pool)
                pool.tensor_copy(kT[:, j % 2, :, 0:W], kT[:, 1 - j % 2, :, P:P + W]).then_inc(kprev_ready, 1)

            def ffn_rstd(u, j):
                pool.wait_ge(mv_ready, u + 1)
                alone(pool)
                pool.tensor_scalar(vpe[:, :], mv[:, 1:2], EPS, None, ALU.add).then_inc(vpe_ready, 1)
                pool.wait_ge(vpe_ready, u + 1)
                pool.tensor_tensor(rstd[:, :], vpe[:, :], nhalf[:, 0:1], ALU.pow).then_inc(rstd_ready, 1)

            def slot(g, gs):
                step(g, gs, 0, keys_before)
                step(g, gs, 0, take_x)
                step(g, gs, 0, carried)
                step(g, gs, 1, ffn_carried)
                step(g, gs, 2, ffn_rstd)
                step(g, gs, 0, norms, 0)
                step(g, gs, 0, norms, 1)
                step(g, gs, 0, sin_part, 0)
                step(g, gs, 0, sin_part, 1)

            pool.wait_ge(a_x1, B)
            pool.wait_ge(zero_ready, 1 + DEPTH * TPB)
            slots(pool, slot)

        @block.vector
        def _(dve):
            dve.wait_ge(ld_const, CONST)
            nc.vector.tensor_copy(identb[:, :], ident[:, :])
            for h in range(HH):
                last = nc.vector.tensor_copy(maskb[:, :, h, :], maskf[:, :, :])
            last.then_inc(mask_ready, 1)
            dve.wait_ge(ld_attn, 160)
            dve.wait_ge(silu_in, 1)
            nc.vector.scalar_tensor_tensor(out=sc[:, 1, :], in0=sc[:, 0, :], scalar=1.0, in1=cT[:, :],
                                           op0=ALU.add, op1=ALU.mult).then_inc(silu_add, 1)
            dve.wait_ge(silu_add, 1)
            nc.vector.tensor_scalar(sc[:, 1, :], sc[:, 1, :], 0.5, None, ALU.mult).then_inc(silu_mul, 1)
            dve.wait_ge(mod_done, 1)
            mod = bank[0][:, 0:6 * B].rearrange("p (i b) -> p i b", i=6)
            for i in (0, 3):
                nc.vector.tensor_copy(modT[:, i, :], mod[:, i, :])
            for i in (1, 4):
                nc.vector.tensor_scalar(modT[:, i, :], mod[:, i, :], 1.0, None, ALU.add)
            for k, i in enumerate((2, 5)):
                nc.vector.tensor_scalar(gt[:, k, :], mod[:, i, :], 0.0, 2.0, ALU.is_ge, ALU.mult).then_inc(silu_mul, 1)
            dve.wait_ge(silu_mul, 3)
            for k, i in enumerate((2, 5)):
                nc.vector.scalar_tensor_tensor(out=modT[:, i, :], in0=gt[:, k, :], scalar=1.0, in1=mod[:, i, :],
                                               op0=ALU.subtract, op1=ALU.mult).then_inc(silu_mul, 1)
            dve.wait_ge(silu_mul, 5)
            for k, i in enumerate((2, 5)):
                nc.vector.tensor_scalar(modT[:, i, :], modT[:, i, :], 0.25, None, ALU.max).then_inc(silu_mul, 1)
            dve.wait_ge(silu_mul, 7)
            for k, i in enumerate((2, 5)):
                last = nc.vector.scalar_tensor_tensor(out=modT[:, i, :], in0=gt[:, k, :], scalar=1.0,
                                                      in1=modT[:, i, :], op0=ALU.subtract, op1=ALU.mult)
            last.then_inc(mod_ready, 1)

            def layernorm4(b, i, src):
                wait(dve, a_norm, 2 * b + i)
                for j in range(TPB):
                    last = nc.vector.bn_stats(ast[:, j, :], src[:, j, :])
                last.then_inc(a_stats, 1)
                wait(dve, a_stats, 2 * b + i + 1)
                wait(dve, a_rstd, 2 * b + i)
                alone(dve)
                for j in range(TPB):
                    last = nc.vector.bn_aggr(amv[:, j, :], ast[:, j, :])
                last.then_inc(a_aggr, 1)
                wait(dve, a_rstd, 2 * b + i + 1)
                wait(dve, a_aggr, 2 * b + i + 1)
                wait(dve, a_nT, 2 * b + i)
                for j in range(TPB):
                    last = nc.vector.tensor_scalar(an[:, j, :], src[:, j, :], amv[:, j, 0:1], ars[:, j:j + 1],
                                                   ALU.subtract, ALU.mult)
                last.then_inc(a_norm, 1)

            def theta(b, j):
                wait(dve, a_act, TPB * b + j + 1)
                nc.vector.scalar_tensor_tensor(out=are[j % 2], in0=ath[j % 2], scalar=0.1, in1=are[j % 2],
                                               op0=ALU.mult, op1=ALU.add).then_inc(a_theta1, 1)
                wait(dve, a_theta1, TPB * b + j + 1)
                nc.vector.scalar_tensor_tensor(out=are[j % 2], in0=ath2[j % 2], scalar=0.15, in1=are[j % 2],
                                               op0=ALU.mult, op1=ALU.add).then_inc(a_theta, 1)
                wait(dve, a_theta, TPB * b + j + 1)
                wait(dve, a_exp, TPB * b)
                nc.vector.tensor_reduce(anm[:, j:j + 1], are[j % 2], AX.X, ALU.max, negate=True).then_inc(a_max, 1)

            def probs(b, j):
                wait(dve, a_exp, TPB * b + j + 1)
                wait(dve, a_prob, TPB * b)
                nc.vector.reciprocal(arc[:, j:j + 1], asum[:, j:j + 1]).then_inc(a_recip, 1)
                wait(dve, a_recip, TPB * b + j + 1)
                nc.vector.tensor_scalar(are[j % 2], are[j % 2], arc[:, j:j + 1], None, ALU.mult).then_inc(a_prob, 1)

            def first_attention(b):
                wait(dve, ld_x, 16 * b + 16)
                layernorm4(b, 0, ax)
                wait(dve, a_proj, 3 * b + 1)
                wait(dve, a_score, TPB * b)
                nc.vector.tensor_scalar(aq, bank[1][:, :], ab[:, 0:1], None, ALU.add).then_inc(a_qs, 1)
                wait(dve, a_proj, 3 * b + 3)
                wait(dve, a_out, b)
                nc.vector.tensor_copy(av, bank[3][:, :].rearrange("p (j f) -> p j f", j=TPB)).then_inc(a_vs, 1)
                theta(b, 0)
                theta(b, 1)
                probs(b, 0)
                probs(b, 1)
                theta(b, 2)
                theta(b, 3)
                probs(b, 2)
                probs(b, 3)
                wait(dve, a_out, b + 1)
                wait(dve, a_y, b)
                nc.vector.tensor_scalar(ao, bank[0][:, :], ab[:, 2:3], None, ALU.add).then_inc(a_outs, 1)
                wait(dve, a_y, b + 1)
                wait(dve, a_yT, b)
                wait(dve, a_cur, b + 1)
                nc.vector.tensor_scalar(ay, bank[1][:, :], ab[:, 3:4], cur[:, 2:3], ALU.add, ALU.mult).then_inc(a_ys, 1)
                wait(dve, a_yT, b + 1)
                wait(dve, a_x1, b)
                nc.vector.tensor_tensor(a2, bank[2][:, :].rearrange("p (j f) -> p j f", j=TPB), ax, ALU.add)\
                    .then_inc(a_x2, 1)
                wait(dve, a_x2, b + 1)
                layernorm4(b, 1, a2)
                wait(dve, a_back, b + 1)
                nc.vector.tensor_copy(Y[:, bass.ds(b * TPB, TPB), :], bank[1][:, :].rearrange("p (j f) -> p j f", j=TPB))\
                    .then_inc(y_ready, TPB)
                nc.vector.tensor_copy(GB[:, bass.ds(b, 1), :], bank[3][:, 0:P].unsqueeze(1)).then_inc(a_gb, 1)

            batches(dve, first_attention)

            def maxes(a, j, h):
                dve.wait_ge(score_done, 2 * a + h + 1)
                wait(dve, sub_ready, 2 * a - 1 + h)
                nc.vector.tensor_reduce(mx[:, h, :], bank[3 + h][:, :].rearrange("p (u k) -> p u k", u=HH),
                                        AX.X, ALU.max).then_inc(max_ready, 1)

            def less_max(a, j, h):
                dve.wait_ge(max_ready, 2 * a + h + 1)
                wait(dve, band_ready, 2 * a - 1 + h)
                wait(dve, prev_ready, 2 * a - 1 + h)
                nc.vector.tensor_tensor(Pr[:, h, :].rearrange("p (u k) -> p u k", u=HH),
                                        bank[3 + h][:, :].rearrange("p (u k) -> p u k", u=HH),
                                        mx[:, h, :].unsqueeze(2).broadcast_to([P, HH, 2 * W]), ALU.subtract)\
                    .then_inc(sub_ready, 1)

            def sums(a, j, h):
                dve.wait_ge(exp_ready, 2 * a + h + 1)
                wait(dve, rsum_ready, 2 * a - 1 + h)
                nc.vector.tensor_reduce(sm[:, h, :], Pr[:, h, :].rearrange("p (u k) -> p u k", u=HH), AX.X, ALU.add)\
                    .then_inc(sum_ready, 1)

            def sums_inverse(a, j, h):
                dve.wait_ge(sum_ready, 2 * a + h + 1)
                wait(dve, prob_ready, 2 * a - 1 + h)
                nc.vector.reciprocal(rs[:, h, :], sm[:, h, :]).then_inc(rsum_ready, 1)

            def probs(a, j, h):
                pr = Pr[:, h, :].rearrange("p (u k) -> p u k", u=HH)
                dve.wait_ge(rsum_ready, 2 * a + h + 1)
                nc.vector.tensor_tensor(pr, pr, rs[:, h, :].unsqueeze(2).broadcast_to([P, HH, 2 * W]), ALU.mult)\
                    .then_inc(prob_ready, 1)

            def probs_before(a, j, h):
                dve.wait_ge(prob_ready, 2 * a + h + 1)
                wait(dve, pv_done, 2 * a - 1 + h)
                nc.vector.transpose(BT[0:W, h, :, :], Pr[0:W, h, :].rearrange("p (u k) -> p u k", u=HH)[:, :, 0:W])\
                    .then_inc(prev_ready, 1)

            def sumsq(n, j, i):
                s = slice(i * HEADS, (i + 1) * HEADS)
                dve.wait_ge(sq_ready, 2 * n + i + 1)
                wait(dve, rr_ready, 2 * n - 1 + i)
                nc.vector.tensor_reduce(ss[:, s], rot[:, i * INNER:(i + 1) * INNER].rearrange("p (h d) -> p h d", d=DH),
                                        AX.X, ALU.add).then_inc(ss_ready, 1)

            def normed(n, j, i):
                q = raw[:, i * INNER:(i + 1) * INNER].rearrange("p (h d) -> p h d", d=DH)
                s = slice(i * HEADS, (i + 1) * HEADS)
                dve.wait_ge(rr_ready, 2 * n + i + 1)
                nc.vector.tensor_tensor(q, q, rr[:, s].unsqueeze(2).broadcast_to([P, HEADS, DH]), ALU.mult)\
                    .then_inc(qn_ready, 1)

            def cos_part(n, j, i):
                q = raw[:, i * INNER:(i + 1) * INNER].rearrange("p (h d) -> p h d", d=DH)
                dve.wait_ge(qn_ready, 2 * n + i + 1)
                tab = TC[:, bass.ds(layer(n), 1), j, i, :]
                nc.vector.tensor_tensor(rot[:, i * INNER:(i + 1) * INNER].rearrange("p (h d) -> p h d", d=DH), q,
                                        tab.broadcast_to([P, HEADS, DH]), ALU.mult).then_inc(cosp_ready, 1)

            def rotated(n, j, i):
                dve.wait_ge(sinp_ready, 2 * n + i + 1)
                dve.wait_ge(cosp_ready, 2 * n + i + 1)
                r = slice(i * INNER, (i + 1) * INNER)
                nc.vector.tensor_tensor(rot[:, r], rot[:, r], swp[:, r], ALU.add).then_inc(rot_ready, 1)

            def ffn_x(u, j):
                dve.wait_ge(wo_done, u + 1)
                dve.wait_ge(y_ready, NT + u)
                nc.vector.tensor_tensor(xf[:, :].unsqueeze(1), bank[6][:, 0:P].unsqueeze(1),
                                        Y[:, bass.ds(u % NT, 1), :], ALU.add).then_inc(xf_ready, 1)

            def ffn_stats(u, j):
                dve.wait_ge(fback_done, u + 1)
                wait(dve, mv_ready, u)
                nc.vector.bn_stats(st[:, :], bank[6][:, 0:P]).then_inc(st_ready, 1)
                dve.wait_ge(st_ready, u + 1)
                wait(dve, rstd_ready, u)
                wait(dve, xn_ready, u)
                alone(dve)
                nc.vector.bn_aggr(mv[:, :], st[:, :]).then_inc(mv_ready, 1)

            def ffn_norm(u, j):
                dve.wait_ge(rstd_ready, u + 1)
                dve.wait_ge(mv_ready, u + 1)
                wait(dve, xnT_done, u)
                nc.vector.tensor_scalar(xn[:, :], bank[6][:, 0:P], mv[:, 0:1], rstd[:, 0:1],
                                        ALU.subtract, ALU.mult).then_inc(xn_ready, 1)

            def gated(u, j):
                dve.wait_ge(ge_ready, u + 1)
                dve.wait_ge(lin_done, u + 1)
                wait(dve, w2_done, u)
                for c, (h0, hn) in enumerate(HC):
                    last = nc.vector.scalar_tensor_tensor(
                        out=hh[0:hn, c, :], in0=bank[6][0:hn, c * P:(c + 1) * P], scalar=b1[0:hn, c:c + 1],
                        in1=ge[0:hn, c, :], op0=ALU.add, op1=ALU.mult)
                last.then_inc(hh_ready, 1)

            def ffn_y(u, j):
                dve.wait_ge(w2_done, u + 1)
                dve.wait_ge(xp_ready, u + 1)
                nc.vector.tensor_tensor(Y[:, bass.ds(u % NT, 1), :], bank[6][:, 0:P].unsqueeze(1),
                                        xf[:, :].unsqueeze(1), ALU.add).then_inc(y_ready, 1)

            def slot(g, gs):
                step(g, gs, 0, sumsq, 0)
                step(g, gs, 1, probs_before, 0)
                step(g, gs, 2, ffn_norm)
                step(g, gs, 1, maxes, 1)
                step(g, gs, 1, less_max, 1)
                step(g, gs, 0, sumsq, 1)
                step(g, gs, 1, sums, 1)
                step(g, gs, 0, normed, 0)
                step(g, gs, 1, sums_inverse, 1)
                step(g, gs, 0, cos_part, 0)
                step(g, gs, 1, probs, 1)
                step(g, gs, 0, normed, 1)
                step(g, gs, 2, gated)
                step(g, gs, 1, probs_before, 1)
                step(g, gs, 0, rotated, 0)
                step(g, gs, 0, cos_part, 1)
                step(g, gs, 0, rotated, 1)
                step(g, gs, 2, ffn_y)
                step(g, gs, 1, ffn_x)
                step(g, gs, 0, maxes, 0)
                step(g, gs, 0, less_max, 0)
                step(g, gs, 1, ffn_stats)
                step(g, gs, 0, sums, 0)
                step(g, gs, 0, sums_inverse, 0)
                step(g, gs, 0, probs, 0)

            slots(dve, slot)

            dve.wait_ge(y_ready, NT + NI)
            dve.wait_ge(a_x1, B)
            for b in range(B):
                yb = Y[:, b * TPB:(b + 1) * TPB, :]
                nc.vector.tensor_tensor(yb, yb, GB[:, b, :].unsqueeze(1).broadcast_to([P, TPB, D]), ALU.mult)\
                    .then_inc(fin_mul, 1)
                wait(dve, fin_mul, b + 1)
                nc.vector.tensor_tensor(yb, yb, X1[:, b * TPB:(b + 1) * TPB, :], ALU.add).then_inc(fin_ready, 1)


def kernel(**inputs):
    import concourse.bacc as bacc
    from concourse.bass_utils import run_bass_kernel_spmd

    f = lambda name: np.asarray(inputs[name])
    tc, ts, mask, eye = tables()
    col = lambda name: f(name).reshape(D, 1)
    arrays = {
        "x": f("L0_attn_x"),
        "wq": f("L0_attn_Wq").T, "wk": f("L0_attn_Wk").T, "wv": f("L0_attn_Wv").T, "wo": f("L0_attn_Wo").T,
        "bq": col("L0_attn_bq"), "bk": col("L0_attn_bk"), "bv": col("L0_attn_bv"), "bo": col("L0_attn_bo"),
        "cT": f("L0_c").T, "wmod": f("L0_wmod").reshape(D, 6, D),
        "wqkv": f("L0_ffn_Wqkv"), "qs": f("L0_ffn_q_scale"), "ks": f("L0_ffn_k_scale"), "fwo": f("L0_ffn_Wo"),
        "ln_g": f("L0_ffn_ln_g").reshape(DEPTH, D, 1), "ln_b": f("L0_ffn_ln_b").reshape(DEPTH, D, 1),
        "w1": f("L0_ffn_W1"), "b1": f("L0_ffn_b1").reshape(DEPTH, 2 * HID, 1),
        "w2": f("L0_ffn_W2"), "b2": f("L0_ffn_b2").reshape(DEPTH, 1, D),
        "tab_cos": tc, "tab_sin": ts, "mask": mask, "eye": eye,
    }
    arrays = {k: np.ascontiguousarray(v) for k, v in arrays.items()}
    nc = bacc.Bacc("TRN2", target_bir_lowering=False, num_devices=1)
    args = [nc.dram_tensor("d_" + k, v.shape, mybir.dt.from_np(v.dtype), kind="ExternalInput").ap()
            for k, v in arrays.items()]
    out = nc.dram_tensor("d_out", (B, S, D), F32, kind="ExternalOutput").ap()
    adaln_block(nc, *args, out)
    r = run_bass_kernel_spmd(nc, [{"d_" + k: v for k, v in arrays.items()}], core_ids=[0])
    return r.results[0]["d_out"]
```

```python
import concourse.bass as bass
from concourse import mybir
from contextlib import ExitStack
import numpy as np

F32 = mybir.dt.float32
BF16 = mybir.dt.bfloat16
ALU = mybir.AluOpType
ACT = mybir.ActivationFunctionType
AX = mybir.AxisListType

B, S, D = 8, 512, 128
DEPTH = 6
HEADS, DH, W = 16, 64, 32
INNER = HEADS * DH
HID = int(D * 4 * 2 / 3)
P = 128
TPB = S // P
NT = B * TPB
NI = DEPTH * NT
NWIN = P // W
HC = [(0, 128), (128, 128), (256, HID - 256)]
NCH = 3 * INNER // 512
HH = HEADS // 2
EPS = 1e-5
MASKED = -1e30


def tables():
    half = np.arange(0, DH, 2, dtype=np.float32)
    inv_freq = (1.0 / 10000.0 ** (half / DH)).astype(np.float32)
    t = np.arange(S, dtype=np.float32)
    freqs = (t[:, None] * inv_freq[None, :]).astype(np.float32)
    freqs = np.concatenate([freqs, freqs], -1).astype(np.float64)
    base = (half + 0.4 * DH) / (1.4 * DH)
    power = (t - S // 2) / (W // 2)
    scale = base[None, :].astype(np.float64) ** power[:, None]
    scale = np.concatenate([scale, scale], -1)
    sign = np.where(np.arange(DH) < DH // 2, -1.0, 1.0)
    cos, sin = np.cos(freqs), np.sin(freqs) * sign
    c = np.stack([cos * scale * 8.0, cos / scale], 1)
    s = np.stack([sin * scale * 8.0, sin / scale], 1)
    c = c.reshape(TPB, P, 2, DH).transpose(1, 0, 2, 3)
    s = s.reshape(TPB, P, 2, DH).transpose(1, 0, 2, 3)
    i = np.arange(P) % W
    w = np.arange(P) // W
    j = np.arange(W)
    prev = np.where(j[None, :] >= i[:, None], 0.0, MASKED)
    own = np.where(j[None, :] <= i[:, None], 0.0, MASKED)
    first = np.where(w[:, None] == 0, MASKED, prev)
    m = np.stack([np.concatenate([prev, own], 1), np.concatenate([first, own], 1)], 1)
    return (np.ascontiguousarray(c, np.float32), np.ascontiguousarray(s, np.float32),
            np.ascontiguousarray(m, np.float32), np.eye(P, dtype=np.float32))


def wait(eng, sem, value):
    if type(value) is int and value <= 0:
        return
    eng.wait_ge(sem, value)


def adaln_block(nc, x_d, wq_d, wk_d, wv_d, wo_d, bq_d, bk_d, bv_d, bo_d, cT_d, wmod_d,
                wqkv_d, qs_d, ks_d, fwo_d, g_d, bln_d, w1_d, b1_d, w2_d, b2_d,
                tc_d, ts_d, mask_d, eye_d, out_d):
    ctx = ExitStack()
    with ctx:
        def sb(name, shape, dt=F32):
            return ctx.enter_context(nc.sbuf_tensor(name, shape, dt))

        def sem(name):
            return ctx.enter_context(nc.semaphore(name))

        X1 = sb("X1", [P, NT, D])
        Y = sb("Y", [P, NT, D])
        GB = sb("GB", [P, B, D])
        ident = sb("ident", [P, P])
        identb = sb("identb", [P, P], BF16)
        maskf = sb("maskf", [P, 2, DH])
        maskb = sb("maskb", [P, 2, HH, DH], BF16)
        TC = sb("TC", [P, DEPTH, TPB, 2, DH])
        TS = sb("TS", [P, DEPTH, TPB, 2, DH])
        qks = sb("qks", [P, DEPTH, 2, DH])
        aw = sb("aw", [P, 4, D])
        ab = sb("ab", [P, 4])
        cT = sb("cT", [P, B])
        sc = sb("sc", [P, 2, B])
        wmod = sb("wmod", [P, 6, D])
        modT = sb("modT", [P, 6, B])
        gt = sb("gt", [P, 2, B])
        cur1 = sb("cur1", [P, 2])
        cur2 = sb("cur2", [P, 4])
        wqkv = sb("wqkv", [P, NCH, 512])
        fwo = sb("fwo", [P, INNER // P, D])
        w1 = sb("w1", [P, 2 * HID])
        w2 = sb("w2", [P, 3, D])
        fv = sb("fv", [P, 2])
        b1 = sb("b1", [P, 6])
        b2 = sb("b2", [1, D])
        ones = sb("ones", [1, P])
        nhalf = sb("nhalf", [P, 2 * HEADS])
        xp = sb("xp", [P, 2, D])
        xs = sb("xs", [P, 2, P + 1])
        raw = sb("raw", [P, 2 * INNER])
        rot = sb("rot", [P, 2 * INNER])
        swp = sb("swp", [P, 2 * INNER])
        ss = sb("ss", [P, 2 * HEADS])
        ssm = sb("ssm", [P, 2 * HEADS])
        rr = sb("rr", [P, 2 * HEADS])
        qT = sb("qT", [P, 2, HH, P])
        kT = sb("kT", [P, 2, HH, W + P])
        V = sb("V", [P, 2, INNER])
        Vp = sb("Vp", [P, 2, INNER])
        mx = sb("mx", [P, 2, HH])
        Pr = sb("Pr", [P, 2, 512])
        PB = sb("PB", [P, 2, HH, P])
        PT = sb("PT", [P, 2, HH, P])
        BT = sb("BT", [P, 2, HH, W])
        sm = sb("sm", [P, 2, HH])
        rs = sb("rs", [P, 2, HH])
        OT = sb("OT", [P, INNER // P, P])
        xf = sb("xf", [P, D])
        fs = sb("fs", [P, 2, P + 1])
        st = sb("st", [P, 6])
        mv = sb("mv", [P, 2])
        vpe = sb("vpe", [P, 1])
        rstd = sb("rstd", [P, 1])
        xn = sb("xn", [P, D])
        xnT = sb("xnT", [P, P])
        ge = sb("ge", [P, 3, P])
        hh = sb("hh", [P, 3, P])
        an = [raw[:, i * 512:(i + 1) * 512].rearrange("p (j f) -> p j f", j=TPB) for i in range(2)]
        ah = raw[:, 1024:1536]
        aq = rot[:, 0:512]
        ak = rot[:, 512:1024]
        av = rot[:, 1024:1536].rearrange("p (j f) -> p j f", j=TPB)
        ao = rot[:, 1536:2048]
        apT = swp[:, :].rearrange("p (t s) -> p t s", t=TPB)
        quarter = lambda buf, i, k: buf[:, i, k:k + 4, :].rearrange("p a b -> p (a b)")
        ath = [quarter(qT, 0, 0), quarter(qT, 1, 0), quarter(PT, 0, 4), quarter(PT, 1, 4)]
        ath2 = [quarter(qT, 0, 4), quarter(qT, 1, 4), raw[:, 1536:2048], sb("ath2", [P, 512])[:, :]]
        are = [Pr[:, 0, :], Pr[:, 1, :]] + [OT[:, k:k + 4, :].rearrange("p a b -> p (a b)") for k in (0, 4)]
        tcb = sb("tcb", [P, TPB, 2, DH])
        tsb = sb("tsb", [P, TPB, 2, DH])
        ast = sb("ast", [P, 2, TPB, 6])
        amv = sb("amv", [P, 2, TPB, 2])
        ave = sb("ave", [P, 2, TPB])
        ars = sb("ars", [P, 2, TPB])
        anm = sb("anm", [P, TPB])
        asum = sb("asum", [P, TPB])
        arc = sb("arc", [P, TPB])
        ay = PT[:, 0, 0:4, :].rearrange("p a b -> p (a b)")
        ah2 = PT[:, 1, 0:4, :].rearrange("p a b -> p (a b)")

        bank = [ctx.enter_context(nc.psum_tensor(f"bank{i}", [P, 512], F32)) for i in range(8)]

        QK_BANK = (2, 5, 2, 5)
        PT_BANK = (3, 4, 3, 4)

        ld_const = sem("ld_const")
        ld_attn = sem("ld_attn")
        ld_x0 = sem("ld_x0")
        ld_x = sem("ld_x")
        wq_loaded = [sem(f"wq_loaded{c}") for c in range(NCH)]
        fwo_loaded = sem("fwo_loaded")
        fw_loaded = sem("fw_loaded")
        vp_moved = sem("vp_moved")
        out_stored = sem("out_stored")
        passed = sem("passed")
        silu_in = sem("silu_in")
        silu_mul = sem("silu_mul")
        mod_done = sem("mod_done")
        mod_ready = sem("mod_ready")
        ones_ready = sem("ones_ready")
        mask_ready = sem("mask_ready")
        silu_add = sem("silu_add")
        zero_ready = sem("zero_ready")
        a_stats = [sem(f"a_stats{i}") for i in range(2)]
        a_aggr = [sem(f"a_aggr{i}") for i in range(2)]
        a_var = [sem(f"a_var{i}") for i in range(2)]
        a_rstd = [sem(f"a_rstd{i}") for i in range(2)]
        a_norm = [sem(f"a_norm{i}") for i in range(2)]
        a_nT = [sem(f"a_nT{i}") for i in range(2)]
        a_cur = [sem(f"a_cur{i}") for i in range(2)]
        a_h = [sem(f"a_h{i}") for i in range(2)]
        a_proj = sem("a_proj")
        a_qs = sem("a_qs")
        a_ks = sem("a_ks")
        a_vs = sem("a_vs")
        a_score = sem("a_score")
        a_act = sem("a_act")
        a_theta1 = sem("a_theta1")
        a_theta = sem("a_theta")
        a_max = sem("a_max")
        a_exp = sem("a_exp")
        a_recip = sem("a_recip")
        a_prob = sem("a_prob")
        a_pT = sem("a_pT")
        a_pTs = sem("a_pTs")
        a_out = sem("a_out")
        a_outs = sem("a_outs")
        a_y = sem("a_y")
        a_ys = sem("a_ys")
        a_yT = sem("a_yT")
        a_x2 = sem("a_x2")
        a_back = sem("a_back")
        a_gb = sem("a_gb")
        y_ready = sem("y_ready")
        xp_ready = sem("xp_ready")
        xT_done = sem("xT_done")
        xs_ready = sem("xs_ready")
        xcol_ready = sem("xcol_ready")
        proj_done = sem("proj_done")
        proj_out = sem("proj_out")
        sq_ready = sem("sq_ready")
        ss_ready = sem("ss_ready")
        ssm_ready = sem("ssm_ready")
        rr_ready = sem("rr_ready")
        qn_ready = sem("qn_ready")
        cosp_ready = sem("cosp_ready")
        sinp_ready = sem("sinp_ready")
        rot_ready = sem("rot_ready")
        qkT_done = sem("qkT_done")
        qkT_out = sem("qkT_out")
        kprev_ready = sem("kprev_ready")
        score_done = sem("score_done")
        max_ready = sem("max_ready")
        sub_ready = sem("sub_ready")
        exp_ready = sem("exp_ready")
        sum_ready = sem("sum_ready")
        rsum_ready = sem("rsum_ready")
        prob_ready = sem("prob_ready")
        prev_ready = sem("prev_ready")
        band_ready = sem("band_ready")
        pT_done = sem("pT_done")
        pT_out = sem("pT_out")
        pv_done = sem("pv_done")
        oT_out = sem("oT_out")
        wo_done = sem("wo_done")
        xf_ready = sem("xf_ready")
        fT_done = sem("fT_done")
        fs_ready = sem("fs_ready")
        fcol_ready = sem("fcol_ready")
        fback_done = sem("fback_done")
        st_ready = sem("st_ready")
        mv_ready = sem("mv_ready")
        vpe_ready = sem("vpe_ready")
        rstd_ready = sem("rstd_ready")
        xn_ready = sem("xn_ready")
        xnT_done = sem("xnT_done")
        xnT_ready = sem("xnT_ready")
        gate_done = sem("gate_done")
        lin_done = sem("lin_done")
        ge_ready = sem("ge_ready")
        hh_ready = sem("hh_ready")
        w2_done = sem("w2_done")
        fin_mul = sem("fin_mul")
        fin_ready = sem("fin_ready")

        LAG = 3
        GROUPS = NI // TPB - 1

        def slots(eng, body):
            for g in range(TPB + LAG):
                body(g, g)
            with eng.Fori(1, GROUPS) as k:
                for i in range(TPB):
                    body(k * TPB + (LAG + i), LAG + i)
            for g in range(TPB * GROUPS + LAG, NI + LAG):
                body(g, g)

        def step(g, gs, lag, do, *part):
            if type(g) is not int or 0 <= g - lag < NI:
                do(g - lag, (gs - lag) % TPB, *part)

        def batch_slots(eng, body):
            for s in range(3):
                body(s)
            with eng.Fori(3, B) as s:
                body(s)
            for s in range(B, B + 2):
                body(s)

        def part(s, lag, do, *which):
            if type(s) is not int or 0 <= s - lag < B:
                do(s - lag, *which)

        def ahead(b):
            return min(b + 2, B) if type(b) is int else b + 2

        block = ctx.enter_context(nc.Block())
        FWL = 12 * 16
        CONST = (4 + 2 * DEPTH) * 16

        def layer(n):
            return n // NT

        def alone(eng):
            eng.sem_inc(passed, 1)

        @block.sync
        def _(sp):
            sp.dma_start(X1[:, 0:TPB, :], x_d[0].rearrange("(j p) f -> p j f", p=P)).then_inc(ld_x0, 16)
            for dst, src in ((ident[:, :], eye_d), (maskf[:, :, :], mask_d),
                             (tcb[:, :, :, :], tc_d), (tsb[:, :, :, :], ts_d)):
                sp.dma_start(dst, src).then_inc(ld_const, 16)
            for l in range(DEPTH):
                for i, s_d in enumerate((qs_d, ks_d)):
                    sp.dma_start(qks[:, l, i, :], s_d[l:l + 1, :].broadcast_to([P, DH])).then_inc(ld_const, 16)
            for i, w_d in enumerate((wq_d, wk_d, wv_d, wo_d)):
                sp.dma_start(aw[:, i, :], w_d).then_inc(ld_attn, 16)
            for i, b_d in enumerate((bq_d, bk_d, bv_d, bo_d)):
                sp.dma_start(ab[:, i:i + 1], b_d).then_inc(ld_attn, 16)
            sp.dma_start(cT[:, :], cT_d).then_inc(ld_attn, 16)
            sp.dma_start(wmod[:, :, :], wmod_d).then_inc(ld_attn, 16)
            sp.dma_start(X1[:, TPB:NT, :].rearrange("p (b j) f -> p b j f", j=TPB),
                         x_d[1:B].rearrange("b (j p) f -> p b j f", p=P)).then_inc(ld_x, 16)

            def shift_v(n, par):
                if type(n) is int and n == 0:
                    sp.wait_ge(zero_ready, 1)
                else:
                    sp.wait_ge(proj_out, n * NCH)
                    alone(sp)
                wait(sp, pv_done, n * 2 - 2)
                alone(sp)
                wait(sp, vp_moved, n * 16)
                alone(sp)
                sp.dma_start(Vp[0:W, par, :], V[P - W:P, 1 - par, :]).then_inc(vp_moved, 16)

            def loads_and_moves(l):
                for c in range(NCH):
                    wait(sp, proj_done, l * (NT * NCH) + (c + 1 - NCH))
                    alone(sp)
                    sp.dma_start(wqkv[:, c, :], wqkv_d[l, :, c * 512:(c + 1) * 512]).then_inc(wq_loaded[c], 16)
                for j in range(2):
                    shift_v(l * NT + j, j % 2)
                wait(sp, wo_done, l * NT)
                alone(sp)
                sp.dma_start(fwo[:, :, :], fwo_d[l].rearrange("(c p) n -> p c n", p=P)).then_inc(fwo_loaded, 16)
                wait(sp, w2_done, l * NT)
                alone(sp)
                sp.dma_start(w1[:, :], w1_d[l]).then_inc(fw_loaded, 16)
                sp.dma_start(w2[:, 0:2, :], w2_d[l, 0:256, :].rearrange("(c p) n -> p c n", p=P)).then_inc(fw_loaded, 16)
                sp.dma_start(w2[0:HID - 256, 2, :], w2_d[l, 256:HID, :]).then_inc(fw_loaded, 16)
                sp.dma_start(fv[:, 0:1], g_d[l]).then_inc(fw_loaded, 16)
                sp.dma_start(fv[:, 1:2], bln_d[l]).then_inc(fw_loaded, 16)
                for i in range(2):
                    for c, (h0, hn) in enumerate(HC):
                        sp.dma_start(b1[0:hn, 3 * i + c:3 * i + c + 1],
                                     b1_d[l, i * HID + h0:i * HID + h0 + hn, :]).then_inc(fw_loaded, 16)
                sp.dma_start(b2[:, :], b2_d[l]).then_inc(fw_loaded, 16)
                for j in range(2, TPB):
                    shift_v(l * NT + j, j % 2)
                with sp.Fori(1, B) as b:
                    for j in range(TPB):
                        shift_v(l * NT + b * TPB + j, j % 2)

            loads_and_moves(0)
            with sp.Fori(1, DEPTH) as l:
                loads_and_moves(l)
            for b in range(B):
                sp.wait_ge(fin_ready, b + 1)
                sp.dma_start(out_d[b].rearrange("(j p) f -> p j f", p=P),
                             Y[:, b * TPB:(b + 1) * TPB, :]).then_inc(out_stored, 16)
            sp.wait_ge(out_stored, 16 * B)

        @block.tensor
        def _(pe):
            pe.wait_ge(ld_attn, 160)
            pe.wait_ge(silu_mul, 1)
            for i in range(6):
                mm = nc.tensor.matmul(bank[0][:, i * B:(i + 1) * B], wmod[:, i, :], sc[:, 1, :], start=True, stop=True)
            mm.then_inc(mod_done, 1)
            pe.wait_ge(ld_const, CONST)
            pe.wait_ge(mod_ready, 1)

            def qkv(b):
                wait(pe, a_h[0], b + 1)
                wait(pe, a_gb, b - 1)
                wait(pe, y_ready, TPB * (b - 1))
                wait(pe, a_h[1], b - 1)
                nc.tensor.matmul(bank[1][:, :], aw[:, 0, :], ah, start=True, stop=True).then_inc(a_proj, 1)
                nc.tensor.matmul(bank[2][:, :], aw[:, 1, :], ah, start=True, stop=True).then_inc(a_proj, 1)
                for j in range(TPB):
                    mm = nc.tensor.matmul(bank[3][:, j * P:(j + 1) * P], ah[:, j * P:(j + 1) * P], aw[:, 2, :],
                                          start=True, stop=True)
                mm.then_inc(a_proj, 1)

            def score_tiles(b):
                wait(pe, a_qs, b + 1)
                wait(pe, a_ks, b + 1)
                wait(pe, a_pTs, TPB * b)
                for j in range(TPB):
                    nc.tensor.matmul(bank[4 + j][:, :], aq[:, j * P:(j + 1) * P], ak, start=True, stop=True)\
                        .then_inc(a_score, 1)

            def tile_back(b, j):
                wait(pe, a_prob, TPB * b + j + 1)
                for u in range(TPB):
                    mm = nc.tensor.transpose(bank[4 + j][:, u * P:(u + 1) * P], are[j][:, u * P:(u + 1) * P],
                                             ident[:, :])
                mm.then_inc(a_pT, 1)

            def weighted(b):
                wait(pe, a_pTs, TPB * (b + 1))
                wait(pe, a_vs, b + 1)
                wait(pe, a_h[0], ahead(b))
                for u in range(TPB):
                    mm = nc.tensor.matmul(bank[0][:, :], av[:, u, :], apT[:, u, :], start=(u == 0), stop=(u == TPB - 1))
                mm.then_inc(a_out, 1)

            def wo(b):
                wait(pe, a_outs, b + 1)
                wait(pe, a_qs, ahead(b))
                wait(pe, a_gb, b)
                nc.tensor.matmul(bank[1][:, :], aw[:, 3, :], ao, start=True, stop=True).then_inc(a_y, 1)

            def y_back(b):
                wait(pe, a_ys, b + 1)
                wait(pe, a_ks, ahead(b))
                wait(pe, y_ready, TPB * b)
                for j in range(TPB):
                    mm = nc.tensor.transpose(bank[2][:, j * P:(j + 1) * P], ay[:, j * P:(j + 1) * P], ident[:, :])
                mm.then_inc(a_yT, 1)

            def norm_back(b, i):
                wait(pe, a_norm[i], b + 1)
                if i == 0:
                    wait(pe, a_outs, b - 1)
                else:
                    wait(pe, a_vs, ahead(b))
                    wait(pe, a_h[1], b)
                for j in range(TPB):
                    mm = nc.tensor.transpose(bank[3 * i][:, j * P:(j + 1) * P], an[i][:, j, :], ident[:, :])
                mm.then_inc(a_nT[i], 1)

            def gate_and_back(b):
                wait(pe, a_ys, b + 1)
                wait(pe, a_cur[1], b + 1)
                nc.tensor.matmul(bank[1][:, 0:P], cur2[:, 3:4].broadcast_to([P, P]), ident[:, :], start=True, stop=True)
                wait(pe, a_h[1], b + 1)
                wait(pe, a_x2, b + 1)
                for j in range(TPB):
                    mm = nc.tensor.transpose(bank[2][:, j * P:(j + 1) * P], ah2[:, j * P:(j + 1) * P], ident[:, :])
                mm.then_inc(a_back, 1)

            def batch_slot(s):
                part(s, 1, qkv)
                part(s, 1, score_tiles)
                part(s, 2, wo)
                part(s, 1, tile_back, 0)
                part(s, 2, y_back)
                part(s, 1, tile_back, 1)
                part(s, 0, norm_back, 0)
                part(s, 1, tile_back, 2)
                part(s, 1, tile_back, 3)
                part(s, 1, weighted)
                part(s, 2, norm_back, 1)
                part(s, 2, gate_and_back)

            batch_slots(pe, batch_slot)

            def x_back(n, j):
                pe.wait_ge(xp_ready, n + 1)
                wait(pe, ge_ready, n - 2)
                nc.tensor.transpose(bank[7][:, 0:P], xp[:, j % 2, :], ident[:, :]).then_inc(xT_done, 1)

            def proj(n, j, c):
                if c == 0:
                    pe.wait_ge(xs_ready, n + 1)
                    pe.wait_ge(xcol_ready, n + 1)
                wait(pe, proj_out, n * NCH + (c - 1))
                if c < 2:
                    wait(pe, oT_out, 2 * n - 3 + c)
                pe.wait_ge(wq_loaded[c], layer(n) * 16 + 16)
                nc.tensor.matmul(bank[c % 2][:, :], xs[:, j % 2, 0:P], wqkv[:, c, :], start=True, stop=True)\
                    .then_inc(proj_done, 1)

            def qk_back(n, j, i):
                pe.wait_ge(rot_ready, 2 * n + i // 2 + 1)
                wait(pe, qkT_out, 4 * n - 1 + i)
                for u in range(4):
                    col = (4 * i + u) * P
                    mm = nc.tensor.transpose(bank[QK_BANK[i]][:, u * P:(u + 1) * P], rot[:, col:col + P], ident[:, :])
                mm.then_inc(qkT_done, 1)

            def scores(a, j, h):
                if h == 0:
                    pe.wait_ge(qkT_out, 4 * a + 4)
                    pe.wait_ge(kprev_ready, a + 1)
                wait(pe, pT_out, 4 * a - 1 + h)
                nc.tensor.matmul(bank[3 + h][:, :], identb[:, :],
                                 maskb[:, 1 if j == 0 else 0, :, :].rearrange("p h k -> p (h k)"),
                                 start=True, stop=False, skip_group_check=True)
                r = slice(h * DH, (h + 1) * DH)
                for w in range(NWIN):
                    for u in range(HH):
                        mm = nc.tensor.matmul(bank[3 + h][w * W:(w + 1) * W, u * DH:(u + 1) * DH],
                                              qT[r, j % 2, u, w * W:(w + 1) * W],
                                              kT[r, j % 2, u, w * W:w * W + 2 * W],
                                              start=False, stop=True, skip_group_check=True)
                mm.then_inc(score_done, 1)

            def probs_back(a, j, i):
                h = i // 2
                pe.wait_ge(band_ready, 2 * a + h + 1)
                if i == 1:
                    pe.wait_ge(sub_ready, 2 * a + 2)
                if i >= 2:
                    pe.wait_ge(pT_out, 4 * a + i - 1)
                for u in range(4):
                    mm = nc.tensor.transpose(bank[PT_BANK[i]][:, u * P:(u + 1) * P],
                                             PB[:, h, 4 * (i % 2) + u, :], ident[:, :])
                mm.then_inc(pT_done, 1)

            def pv(a, j, h):
                pe.wait_ge(pT_out, 4 * a + 2 * h + 2)
                pe.wait_ge(prev_ready, 2 * a + h + 1)
                pe.wait_ge(vp_moved, 16 * a + 16)
                ahead = min(a + 2, NI) if type(a) is int else a + 2
                pe.wait_ge(proj_out, NCH * ahead)
                for u in range(HH):
                    hc = (2 * u + h) * DH
                    dst = bank[u // 4][h * DH:(h + 1) * DH, (u % 4) * P:(u % 4 + 1) * P]
                    nc.tensor.matmul(dst, V[:, j % 2, hc:hc + DH], PT[:, h, u, :], start=True, stop=False,
                                     skip_group_check=True)
                    mm = nc.tensor.matmul(dst[:, 0:W], Vp[:, j % 2, hc:hc + DH], BT[:, h, u, :], start=False,
                                          stop=True, skip_group_check=True)
                mm.then_inc(pv_done, 1)

            def out_proj(u, j):
                pe.wait_ge(oT_out, 2 * u + 2)
                pe.wait_ge(y_ready, NT + u)
                pe.wait_ge(fwo_loaded, layer(u) * 16 + 16)
                for c in range(INNER // P):
                    mm = nc.tensor.matmul(bank[6][:, 0:P], OT[:, c, :], fwo[:, c, :],
                                          start=(c == 0), stop=(c == INNER // P - 1))
                mm.then_inc(wo_done, 1)

            def ffn_x_back(u, j):
                pe.wait_ge(xf_ready, u + 1)
                pe.wait_ge(xs_ready, min(u + 3, NI) if type(u) is int else u + 3)
                wait(pe, ge_ready, u)
                nc.tensor.transpose(bank[7][:, 0:P], xf[:, :], ident[:, :]).then_inc(fT_done, 1)

            def ffn_x_forth(u, j):
                pe.wait_ge(fs_ready, u + 1)
                pe.wait_ge(fcol_ready, u + 1)
                nc.tensor.transpose(bank[6][:, 0:P], fs[:, j % 2, 0:P], ident[:, :]).then_inc(fback_done, 1)

            def ffn_norm_back(u, j):
                pe.wait_ge(xn_ready, u + 1)
                pe.wait_ge(fw_loaded, layer(u) * FWL + FWL)
                nc.tensor.transpose(bank[7][:, 0:P], xn[:, :], ident[:, :]).then_inc(xnT_done, 1)

            def ffn_in(u, j, i):
                pe.wait_ge(xnT_ready, u + 1)
                bk, done = ((bank[6], lin_done), (bank[7], gate_done))[i]
                for c, (h0, hn) in enumerate(HC):
                    mm = nc.tensor.matmul(bk[0:hn, c * P:(c + 1) * P], w1[:, i * HID + h0:i * HID + h0 + hn],
                                          xnT[:, :], start=True, stop=True)
                mm.then_inc(done, 1)

            def ffn_out(u, j):
                pe.wait_ge(hh_ready, u + 1)
                for c, (h0, hn) in enumerate(HC):
                    nc.tensor.matmul(bank[6][:, 0:P], hh[0:hn, c, :], w2[0:hn, c, :], start=(c == 0), stop=False)
                nc.tensor.matmul(bank[6][:, 0:P], ones[:, :], b2[:, :], start=False, stop=True).then_inc(w2_done, 1)

            def slot(g, gs):
                step(g, gs, 2, probs_back, 1)
                step(g, gs, 3, ffn_x_back)
                step(g, gs, 1, proj, 5)
                step(g, gs, 3, ffn_x_forth)
                step(g, gs, 2, pv, 0)
                step(g, gs, 3, ffn_norm_back)
                step(g, gs, 2, probs_back, 2)
                step(g, gs, 2, probs_back, 3)
                step(g, gs, 3, ffn_in, 1)
                step(g, gs, 3, ffn_in, 0)
                step(g, gs, 2, pv, 1)
                step(g, gs, 1, qk_back, 0)
                step(g, gs, 0, x_back)
                step(g, gs, 1, qk_back, 1)
                step(g, gs, 0, proj, 0)
                step(g, gs, 1, qk_back, 2)
                step(g, gs, 1, qk_back, 3)
                step(g, gs, 0, proj, 1)
                step(g, gs, 1, scores, 0)
                step(g, gs, 0, proj, 2)
                step(g, gs, 0, proj, 3)
                step(g, gs, 1, scores, 1)
                step(g, gs, 3, ffn_out)
                step(g, gs, 0, proj, 4)
                step(g, gs, 2, out_proj)
                step(g, gs, 1, probs_back, 0)

            pe.wait_ge(ones_ready, 1)
            pe.wait_ge(mask_ready, 1)
            pe.wait_ge(a_gb, B)
            slots(pe, slot)

        @block.scalar
        def _(act):
            act.wait_ge(ld_attn, 160)
            nc.scalar.activation(sc[:, 0, :], cT[:, :], ACT.Tanh, scale=0.5).then_inc(silu_in, 1)

            def theta_parts(b, j):
                wait(act, a_score, TPB * b + j + 1)
                wait(act, a_theta, TPB * b)
                wait(act, a_pT, TPB * b)
                nc.scalar.activation(ath[j], bank[4 + j][:, :], ACT.Tanh, scale=0.5)
                nc.scalar.activation(ath2[j], bank[4 + j][:, :], ACT.Tanh)
                nc.scalar.activation(are[j], bank[4 + j][:, :], ACT.Relu, scale=0.1).then_inc(a_act, 1)

            def exps(b, j):
                wait(act, a_max, TPB * b + j + 1)
                nc.scalar.activation(are[j], are[j], ACT.Exp, bias=anm[:, j:j + 1],
                                     accum_out=asum[:, j:j + 1]).then_inc(a_exp, 1)

            def probs_out(b, j):
                if j == 0:
                    wait(act, a_out, b)
                wait(act, a_pT, TPB * b + j + 1)
                nc.scalar.activation(apT[:, :, j * P:(j + 1) * P],
                                     bank[4 + j][:, :].rearrange("p (u s) -> p u s", u=TPB), ACT.Copy)\
                    .then_inc(a_pTs, 1)

            def modulated(b):
                wait(act, a_nT[0], b + 1)
                wait(act, a_cur[0], b + 1)
                wait(act, a_proj, 3 * b)
                nc.scalar.activation(ah, bank[0][:, :], ACT.Identity, scale=cur1[:, 1:2], bias=cur1[:, 0:1])\
                    .then_inc(a_h[0], 1)

            def k_out(b):
                wait(act, a_proj, 3 * b + 2)
                wait(act, a_score, TPB * b)
                nc.scalar.activation(ak, bank[2][:, :], ACT.Identity, bias=ab[:, 1:2], scale=1.0).then_inc(a_ks, 1)

            def modulated2(b):
                wait(act, a_nT[1], b + 1)
                wait(act, a_cur[1], b + 1)
                wait(act, a_back, b)
                nc.scalar.activation(ah2, bank[3][:, :], ACT.Identity, scale=cur2[:, 2:3], bias=cur2[:, 1:2])\
                    .then_inc(a_h[1], 1)

            def batch_slot(s):
                part(s, 1, k_out)
                part(s, 1, theta_parts, 0)
                part(s, 1, theta_parts, 1)
                part(s, 1, theta_parts, 2)
                part(s, 1, theta_parts, 3)
                part(s, 1, exps, 0)
                part(s, 1, exps, 1)
                part(s, 1, probs_out, 0)
                part(s, 1, exps, 2)
                part(s, 1, probs_out, 1)
                part(s, 0, modulated)
                part(s, 1, exps, 3)
                part(s, 1, probs_out, 2)
                part(s, 1, probs_out, 3)
                part(s, 2, modulated2)

            batch_slots(act, batch_slot)

            def shifted(n, j):
                act.wait_ge(xT_done, n + 1)
                wait(act, xcol_ready, n)
                wait(act, proj_done, NCH * (n - 1))
                nc.scalar.activation(xs[0:64, j % 2, 0:P], bank[7][0:64, 0:P], ACT.Copy)
                nc.scalar.activation(xs[64:P, j % 2, 1:P + 1], bank[7][64:P, 0:P], ACT.Copy).then_inc(xs_ready, 1)

            def to_raw(n, j, c):
                act.wait_ge(proj_done, NCH * n + c + 1)
                if c % 2 == 0:
                    wait(act, sinp_ready, 2 * n - 1 + c // 2)
                    wait(act, cosp_ready, 2 * n - 1 + c // 2)
                nc.scalar.activation(raw[:, c * 512:(c + 1) * 512], bank[c % 2][:, :], ACT.Copy).then_inc(proj_out, 1)

            def squares(n, j, i):
                act.wait_ge(proj_out, NCH * n + 2 * i + 2)
                wait(act, qkT_done, 4 * n - 2 + 2 * i)
                nc.scalar.activation(rot[:, i * INNER:(i + 1) * INNER], raw[:, i * INNER:(i + 1) * INNER],
                                     ACT.Square).then_inc(sq_ready, 1)

            def to_v(n, j, c):
                act.wait_ge(proj_done, NCH * n + c + 1)
                if c == 4:
                    wait(act, pv_done, 2 * n - 2)
                    wait(act, vp_moved, 16 * n)
                nc.scalar.activation(V[:, j % 2, (c - 4) * 512:(c - 3) * 512], bank[c % 2][:, :], ACT.Copy)\
                    .then_inc(proj_out, 1)

            def qk_to_sbuf(n, j, i):
                act.wait_ge(qkT_done, 4 * n + i + 1)
                wait(act, score_done, 2 * n - 2)
                if i < 2:
                    dst = qT[:, j % 2, 4 * i:4 * i + 4, :]
                else:
                    wait(act, kprev_ready, n)
                    dst = kT[:, j % 2, 4 * i - 8:4 * i - 4, W:W + P]
                nc.scalar.activation(dst, bank[QK_BANK[i]][:, :].rearrange("p (c s) -> p c s", c=4), ACT.Copy)\
                    .then_inc(qkT_out, 1)

            def exp_half(a, j, h):
                act.wait_ge(sub_ready, 2 * a + h + 1)
                nc.scalar.activation(Pr[:, h, :], Pr[:, h, :], ACT.Exp).then_inc(exp_ready, 1)

            def to_band(a, j, h):
                act.wait_ge(prob_ready, 2 * a + h + 1)
                wait(act, pT_done, 4 * a - 2 + 2 * h)
                src = Pr[:, h, :].rearrange("p (u k) -> p u k", u=HH)
                nc.scalar.activation(PB[0:W, h, :, 0:W], src[0:W, :, W:2 * W], ACT.Copy)
                for w in range(1, NWIN):
                    r = slice(w * W, (w + 1) * W)
                    last = nc.scalar.activation(PB[r, h, :, (w - 1) * W:(w + 1) * W], src[r, :, :], ACT.Copy)
                last.then_inc(band_ready, 1)

            def probs_to_sbuf(a, j, i):
                act.wait_ge(pT_done, 4 * a + i + 1)
                wait(act, pv_done, 2 * a - 1 + i // 2)
                nc.scalar.activation(PT[:, i // 2, 4 * (i % 2):4 * (i % 2) + 4, :],
                                     bank[PT_BANK[i]][:, :].rearrange("p (c s) -> p c s", c=4), ACT.Copy)\
                    .then_inc(pT_out, 1)

            def o_to_sbuf(a, j, i):
                act.wait_ge(pv_done, 2 * a + 2)
                wait(act, wo_done, a)
                nc.scalar.activation(OT[:, 4 * i:4 * i + 4, :], bank[i][:, :].rearrange("p (c s) -> p c s", c=4),
                                     ACT.Copy).then_inc(oT_out, 1)

            def ffn_shifted(u, j):
                act.wait_ge(fT_done, u + 1)
                wait(act, fcol_ready, u)
                nc.scalar.activation(fs[0:64, j % 2, 0:P], bank[7][0:64, 0:P], ACT.Copy)
                nc.scalar.activation(fs[64:P, j % 2, 1:P + 1], bank[7][64:P, 0:P], ACT.Copy).then_inc(fs_ready, 1)

            def ffn_affine(u, j):
                act.wait_ge(xnT_done, u + 1)
                nc.scalar.activation(xnT[:, :], bank[7][:, 0:P], ACT.Identity, scale=fv[:, 0:1], bias=fv[:, 1:2])\
                    .then_inc(xnT_ready, 1)

            def gelu(u, j):
                act.wait_ge(gate_done, u + 1)
                wait(act, hh_ready, u)
                for c, (h0, hn) in enumerate(HC):
                    last = nc.scalar.activation(ge[0:hn, c, :], bank[7][0:hn, c * P:(c + 1) * P], ACT.Gelu,
                                                bias=b1[0:hn, 3 + c:4 + c], scale=1.0)
                last.then_inc(ge_ready, 1)

            def slot(g, gs):
                step(g, gs, 1, squares, 0)
                step(g, gs, 2, exp_half, 0)
                step(g, gs, 1, to_raw, 2)
                step(g, gs, 1, to_raw, 3)
                step(g, gs, 1, squares, 1)
                step(g, gs, 2, to_band, 0)
                step(g, gs, 2, exp_half, 1)
                step(g, gs, 1, to_v, 4)
                step(g, gs, 2, probs_to_sbuf, 0)
                step(g, gs, 3, ffn_shifted)
                step(g, gs, 2, probs_to_sbuf, 1)
                step(g, gs, 1, to_v, 5)
                step(g, gs, 2, to_band, 1)
                step(g, gs, 3, ffn_affine)
                step(g, gs, 2, probs_to_sbuf, 2)
                step(g, gs, 2, probs_to_sbuf, 3)
                step(g, gs, 3, gelu)
                step(g, gs, 2, o_to_sbuf, 0)
                step(g, gs, 0, shifted)
                step(g, gs, 1, qk_to_sbuf, 0)
                step(g, gs, 1, qk_to_sbuf, 1)
                step(g, gs, 2, o_to_sbuf, 1)
                step(g, gs, 1, qk_to_sbuf, 2)
                step(g, gs, 1, qk_to_sbuf, 3)
                step(g, gs, 0, to_raw, 0)
                step(g, gs, 0, to_raw, 1)

            slots(act, slot)

        @block.gpsimd
        def _(pool):
            pool.memset(ones[:, :], 1.0)
            pool.memset(nhalf[:, :], -0.5).then_inc(ones_ready, 1)
            pool.memset(kT[:, :, :, :], 0.0)
            pool.memset(PB[:, :, :, :], 0.0)
            pool.memset(BT[:, :, :, :], 0.0)
            pool.memset(Vp[:, :, :], 0.0)
            pool.memset(V[:, :, :], 0.0).then_inc(zero_ready, 1)
            pool.wait_ge(ones_ready, 1)
            pool.wait_ge(ld_const, CONST)
            for l in range(DEPTH):
                for j in range(TPB):
                    pool.tensor_tensor(TC[:, l, j, :, :], tcb[:, j, :, :], qks[:, l, :, :], ALU.mult)
                    pool.tensor_tensor(TS[:, l, j, :, 0:32], tsb[:, j, :, 0:32], qks[:, l, :, 32:64], ALU.mult)
                    pool.tensor_tensor(TS[:, l, j, :, 32:64], tsb[:, j, :, 32:64], qks[:, l, :, 0:32], ALU.mult)\
                        .then_inc(zero_ready, 1)

            pool.wait_ge(mod_ready, 1)

            def columns(b, i):
                wait(pool, a_h[i], b)
                if i == 1:
                    wait(pool, a_ys, b)
                    wait(pool, a_back, b)
                alone(pool)
                dst = (cur1, cur2)[i][:, :].unsqueeze(2)
                pool.tensor_copy(dst, modT[:, 2 * i:2 + 4 * i, bass.ds(b, 1)]).then_inc(a_cur[i], 1)

            def rstd4(b, i):
                wait(pool, a_aggr[i], b + 1)
                wait(pool, a_norm[i], b)
                alone(pool)
                pool.tensor_scalar(ave[:, i, :], amv[:, i, :, 1], EPS, None, ALU.add).then_inc(a_var[i], 1)
                wait(pool, a_var[i], b + 1)
                pool.tensor_tensor(ars[:, i, :], ave[:, i, :], nhalf[:, 0:TPB], ALU.pow).then_inc(a_rstd[i], 1)

            def batch_slot(s):
                part(s, 0, columns, 0)
                part(s, 0, rstd4, 0)
                part(s, 2, columns, 1)
                part(s, 2, rstd4, 1)

            batch_slots(pool, batch_slot)

            def take_x(n, j):
                pool.wait_ge(y_ready, n + 1)
                wait(pool, xT_done, n - 1)
                alone(pool)
                pool.tensor_copy(xp[:, j % 2, :].unsqueeze(1), Y[:, bass.ds(n % NT, 1), :]).then_inc(xp_ready, 1)

            def carried(n, j):
                wait(pool, proj_done, NCH * (n - 1))
                wait(pool, xs_ready, n)
                pool.wait_ge(xp_ready, n + 1)
                wait(pool, rr_ready, 2 * n)
                wait(pool, rstd_ready, n - 2)
                alone(pool)
                if j == 0:
                    pool.memset(xs[64:P, 0, 0:1], 0.0).then_inc(xcol_ready, 1)
                else:
                    pool.tensor_copy(xs[64:P, j % 2, 0:1], xs[64:P, 1 - j % 2, P:P + 1]).then_inc(xcol_ready, 1)
                pool.wait_ge(xcol_ready, n + 1)

            def ffn_carried(u, j):
                wait(pool, fback_done, u - 1)
                wait(pool, fs_ready, u)
                wait(pool, rstd_ready, u)
                wait(pool, kprev_ready, min(u + 3, NI) if type(u) is int else u + 3)
                wait(pool, sinp_ready, min(2 * u + 4, 2 * NI) if type(u) is int else 2 * u + 4)
                alone(pool)
                if j == 0:
                    pool.memset(fs[64:P, 0, 0:1], 0.0).then_inc(fcol_ready, 1)
                else:
                    pool.tensor_copy(fs[64:P, j % 2, 0:1], fs[64:P, 1 - j % 2, P:P + 1]).then_inc(fcol_ready, 1)
                pool.wait_ge(fcol_ready, u + 1)

            def norms(n, j, i):
                s = slice(i * HEADS, (i + 1) * HEADS)
                pool.wait_ge(ss_ready, 2 * n + i + 1)
                wait(pool, qn_ready, 2 * n - 1 + i)
                alone(pool)
                pool.tensor_scalar(ssm[:, s], ss[:, s], 1e-24, None, ALU.max).then_inc(ssm_ready, 1)
                pool.wait_ge(ssm_ready, 2 * n + i + 1)
                pool.tensor_tensor(rr[:, s], ssm[:, s], nhalf[:, s], ALU.pow).then_inc(rr_ready, 1)

            def sin_part(n, j, i):
                pool.wait_ge(qn_ready, 2 * n + i + 1)
                wait(pool, rot_ready, 2 * n - 1 + i)
                src = raw[:, i * INNER:(i + 1) * INNER].rearrange("p (h t d) -> p h t d", t=2, d=32)
                dst = swp[:, i * INNER:(i + 1) * INNER].rearrange("p (h t d) -> p h t d", t=2, d=32)
                for t in range(2):
                    tab = TS[:, bass.ds(layer(n), 1), j, i, 32 * t:32 * t + 32]
                    last = pool.tensor_tensor(dst[:, :, t, :], src[:, :, 1 - t, :],
                                              tab.broadcast_to([P, HEADS, 32]), ALU.mult)
                last.then_inc(sinp_ready, 1)

            def keys_before(n, j):
                wait(pool, qkT_out, 4 * n)
                wait(pool, score_done, 2 * n - 2)
                alone(pool)
                pool.tensor_copy(kT[:, j % 2, :, 0:W], kT[:, 1 - j % 2, :, P:P + W]).then_inc(kprev_ready, 1)

            def ffn_rstd(u, j):
                pool.wait_ge(mv_ready, u + 1)
                alone(pool)
                pool.tensor_scalar(vpe[:, :], mv[:, 1:2], EPS, None, ALU.add).then_inc(vpe_ready, 1)
                pool.wait_ge(vpe_ready, u + 1)
                pool.tensor_tensor(rstd[:, :], vpe[:, :], nhalf[:, 0:1], ALU.pow).then_inc(rstd_ready, 1)

            def slot(g, gs):
                step(g, gs, 0, take_x)
                step(g, gs, 1, norms, 1)
                step(g, gs, 3, ffn_rstd)
                step(g, gs, 0, carried)
                step(g, gs, 1, sin_part, 0)
                step(g, gs, 1, sin_part, 1)
                step(g, gs, 0, keys_before)
                step(g, gs, 2, ffn_carried)
                step(g, gs, 0, norms, 0)

            pool.wait_ge(zero_ready, 1 + DEPTH * TPB)
            slots(pool, slot)

        @block.vector
        def _(dve):
            dve.wait_ge(ld_const, CONST)
            nc.vector.tensor_copy(identb[:, :], ident[:, :])
            for h in range(HH):
                last = nc.vector.tensor_copy(maskb[:, :, h, :], maskf[:, :, :])
            last.then_inc(mask_ready, 1)
            dve.wait_ge(ld_attn, 160)
            dve.wait_ge(silu_in, 1)
            nc.vector.scalar_tensor_tensor(out=sc[:, 1, :], in0=sc[:, 0, :], scalar=1.0, in1=cT[:, :],
                                           op0=ALU.add, op1=ALU.mult).then_inc(silu_add, 1)
            dve.wait_ge(silu_add, 1)
            nc.vector.tensor_scalar(sc[:, 1, :], sc[:, 1, :], 0.5, None, ALU.mult).then_inc(silu_mul, 1)
            dve.wait_ge(mod_done, 1)
            mod = bank[0][:, 0:6 * B].rearrange("p (i b) -> p i b", i=6)
            for i in (0, 3):
                nc.vector.tensor_copy(modT[:, i, :], mod[:, i, :])
            for i in (1, 4):
                nc.vector.tensor_scalar(modT[:, i, :], mod[:, i, :], 1.0, None, ALU.add)
            for k, i in enumerate((2, 5)):
                nc.vector.tensor_scalar(gt[:, k, :], mod[:, i, :], 0.0, 2.0, ALU.is_ge, ALU.mult).then_inc(silu_mul, 1)
            dve.wait_ge(silu_mul, 3)
            for k, i in enumerate((2, 5)):
                nc.vector.scalar_tensor_tensor(out=modT[:, i, :], in0=gt[:, k, :], scalar=1.0, in1=mod[:, i, :],
                                               op0=ALU.subtract, op1=ALU.mult).then_inc(silu_mul, 1)
            dve.wait_ge(silu_mul, 5)
            for k, i in enumerate((2, 5)):
                nc.vector.tensor_scalar(modT[:, i, :], modT[:, i, :], 0.25, None, ALU.max).then_inc(silu_mul, 1)
            dve.wait_ge(silu_mul, 7)
            for k, i in enumerate((2, 5)):
                last = nc.vector.scalar_tensor_tensor(out=modT[:, i, :], in0=gt[:, k, :], scalar=1.0,
                                                      in1=modT[:, i, :], op0=ALU.subtract, op1=ALU.mult)
            last.then_inc(mod_ready, 1)

            def tile_of(b, j):
                return X1[:, bass.ds(b * TPB + j, 1), :]

            def stats4(b, i):
                if i == 1:
                    wait(dve, a_x2, b + 1)
                elif type(b) is int and b == 0:
                    wait(dve, ld_x0, 16)
                else:
                    wait(dve, ld_x, 16)
                wait(dve, a_aggr[i], b)
                alone(dve)
                for j in range(TPB):
                    last = nc.vector.bn_stats(ast[:, i, j, :].unsqueeze(1), tile_of(b, j))
                last.then_inc(a_stats[i], 1)
                wait(dve, a_stats[i], b + 1)
                wait(dve, a_rstd[i], b)
                wait(dve, a_norm[i], b)
                alone(dve)
                for j in range(TPB):
                    last = nc.vector.bn_aggr(amv[:, i, j, :], ast[:, i, j, :])
                last.then_inc(a_aggr[i], 1)

            def norm4(b, i):
                wait(dve, a_rstd[i], b + 1)
                wait(dve, a_aggr[i], b + 1)
                wait(dve, a_nT[i], b)
                for j in range(TPB):
                    last = nc.vector.tensor_scalar(an[i][:, j:j + 1, :], tile_of(b, j), amv[:, i, j, 0:1],
                                                   ars[:, i, j:j + 1], ALU.subtract, ALU.mult)
                last.then_inc(a_norm[i], 1)

            def theta(b, j):
                wait(dve, a_act, TPB * b + j + 1)
                nc.vector.scalar_tensor_tensor(out=are[j], in0=ath[j], scalar=0.1, in1=are[j],
                                               op0=ALU.mult, op1=ALU.add).then_inc(a_theta1, 1)
                wait(dve, a_theta1, TPB * b + j + 1)
                nc.vector.scalar_tensor_tensor(out=are[j], in0=ath2[j], scalar=0.15, in1=are[j],
                                               op0=ALU.mult, op1=ALU.add).then_inc(a_theta, 1)
                wait(dve, a_theta, TPB * b + j + 1)
                wait(dve, a_exp, TPB * b)
                nc.vector.tensor_reduce(anm[:, j:j + 1], are[j], AX.X, ALU.max, negate=True).then_inc(a_max, 1)

            def attn_probs(b, j):
                wait(dve, a_exp, TPB * b + j + 1)
                wait(dve, a_prob, TPB * b)
                nc.vector.reciprocal(arc[:, j:j + 1], asum[:, j:j + 1]).then_inc(a_recip, 1)
                wait(dve, a_recip, TPB * b + j + 1)
                nc.vector.tensor_scalar(are[j], are[j], arc[:, j:j + 1], None, ALU.mult).then_inc(a_prob, 1)

            def q_out(b):
                wait(dve, a_proj, 3 * b + 1)
                wait(dve, a_score, TPB * b)
                nc.vector.tensor_scalar(aq, bank[1][:, :], ab[:, 0:1], None, ALU.add).then_inc(a_qs, 1)

            def v_out(b):
                wait(dve, a_proj, 3 * b + 3)
                wait(dve, a_out, b)
                nc.vector.tensor_copy(av, bank[3][:, :].rearrange("p (j f) -> p j f", j=TPB)).then_inc(a_vs, 1)

            def with_bias(b):
                wait(dve, a_out, b + 1)
                wait(dve, a_y, b)
                nc.vector.tensor_scalar(ao, bank[0][:, :], ab[:, 2:3], None, ALU.add).then_inc(a_outs, 1)

            def gated_y(b):
                wait(dve, a_y, b + 1)
                wait(dve, a_yT, b)
                wait(dve, a_cur[1], b + 1)
                nc.vector.tensor_scalar(ay, bank[1][:, :], ab[:, 3:4], cur2[:, 0:1], ALU.add, ALU.mult).then_inc(a_ys, 1)

            def x_after(b):
                wait(dve, a_yT, b + 1)
                wait(dve, a_norm[0], b + 1)
                xb = X1[:, bass.ds(b * TPB, TPB), :]
                nc.vector.tensor_tensor(xb, bank[2][:, :].rearrange("p (j f) -> p j f", j=TPB), xb, ALU.add)\
                    .then_inc(a_x2, 1)

            def y_and_gate(b):
                wait(dve, a_back, b + 1)
                nc.vector.tensor_copy(Y[:, bass.ds(b * TPB, TPB), :], bank[2][:, :].rearrange("p (j f) -> p j f", j=TPB))\
                    .then_inc(y_ready, TPB)
                nc.vector.tensor_copy(GB[:, bass.ds(b, 1), :], bank[1][:, 0:P].unsqueeze(1)).then_inc(a_gb, 1)

            def batch_slot(s):
                part(s, 1, q_out)
                part(s, 1, v_out)
                part(s, 0, stats4, 0)
                part(s, 1, theta, 0)
                part(s, 2, gated_y)
                part(s, 1, theta, 1)
                part(s, 1, attn_probs, 0)
                part(s, 1, theta, 2)
                part(s, 1, attn_probs, 1)
                part(s, 2, x_after)
                part(s, 1, theta, 3)
                part(s, 0, norm4, 0)
                part(s, 1, attn_probs, 2)
                part(s, 2, stats4, 1)
                part(s, 1, attn_probs, 3)
                part(s, 2, norm4, 1)
                part(s, 1, with_bias)
                part(s, 2, y_and_gate)

            batch_slots(dve, batch_slot)

            def maxes(a, j, h):
                dve.wait_ge(score_done, 2 * a + h + 1)
                wait(dve, sub_ready, 2 * a - 1 + h)
                nc.vector.tensor_reduce(mx[:, h, :], bank[3 + h][:, :].rearrange("p (u k) -> p u k", u=HH),
                                        AX.X, ALU.max).then_inc(max_ready, 1)

            def less_max(a, j, h):
                dve.wait_ge(max_ready, 2 * a + h + 1)
                wait(dve, band_ready, 2 * a - 1 + h)
                wait(dve, prev_ready, 2 * a - 1 + h)
                nc.vector.tensor_tensor(Pr[:, h, :].rearrange("p (u k) -> p u k", u=HH),
                                        bank[3 + h][:, :].rearrange("p (u k) -> p u k", u=HH),
                                        mx[:, h, :].unsqueeze(2).broadcast_to([P, HH, 2 * W]), ALU.subtract)\
                    .then_inc(sub_ready, 1)

            def sums(a, j, h):
                dve.wait_ge(exp_ready, 2 * a + h + 1)
                wait(dve, rsum_ready, 2 * a - 1 + h)
                nc.vector.tensor_reduce(sm[:, h, :], Pr[:, h, :].rearrange("p (u k) -> p u k", u=HH), AX.X, ALU.add)\
                    .then_inc(sum_ready, 1)

            def sums_inverse(a, j, h):
                dve.wait_ge(sum_ready, 2 * a + h + 1)
                wait(dve, prob_ready, 2 * a - 1 + h)
                nc.vector.reciprocal(rs[:, h, :], sm[:, h, :]).then_inc(rsum_ready, 1)

            def probs(a, j, h):
                pr = Pr[:, h, :].rearrange("p (u k) -> p u k", u=HH)
                dve.wait_ge(rsum_ready, 2 * a + h + 1)
                nc.vector.tensor_tensor(pr, pr, rs[:, h, :].unsqueeze(2).broadcast_to([P, HH, 2 * W]), ALU.mult)\
                    .then_inc(prob_ready, 1)

            def probs_before(a, j, h):
                dve.wait_ge(prob_ready, 2 * a + h + 1)
                wait(dve, pv_done, 2 * a - 1 + h)
                nc.vector.transpose(BT[0:W, h, :, :], Pr[0:W, h, :].rearrange("p (u k) -> p u k", u=HH)[:, :, 0:W])\
                    .then_inc(prev_ready, 1)

            def sumsq(n, j, i):
                s = slice(i * HEADS, (i + 1) * HEADS)
                dve.wait_ge(sq_ready, 2 * n + i + 1)
                wait(dve, rr_ready, 2 * n - 1 + i)
                nc.vector.tensor_reduce(ss[:, s], rot[:, i * INNER:(i + 1) * INNER].rearrange("p (h d) -> p h d", d=DH),
                                        AX.X, ALU.add).then_inc(ss_ready, 1)

            def normed(n, j, i):
                q = raw[:, i * INNER:(i + 1) * INNER].rearrange("p (h d) -> p h d", d=DH)
                s = slice(i * HEADS, (i + 1) * HEADS)
                dve.wait_ge(rr_ready, 2 * n + i + 1)
                nc.vector.tensor_tensor(q, q, rr[:, s].unsqueeze(2).broadcast_to([P, HEADS, DH]), ALU.mult)\
                    .then_inc(qn_ready, 1)

            def cos_part(n, j, i):
                q = raw[:, i * INNER:(i + 1) * INNER].rearrange("p (h d) -> p h d", d=DH)
                dve.wait_ge(qn_ready, 2 * n + i + 1)
                tab = TC[:, bass.ds(layer(n), 1), j, i, :]
                nc.vector.tensor_tensor(rot[:, i * INNER:(i + 1) * INNER].rearrange("p (h d) -> p h d", d=DH), q,
                                        tab.broadcast_to([P, HEADS, DH]), ALU.mult).then_inc(cosp_ready, 1)

            def rotated(n, j, i):
                dve.wait_ge(sinp_ready, 2 * n + i + 1)
                dve.wait_ge(cosp_ready, 2 * n + i + 1)
                r = slice(i * INNER, (i + 1) * INNER)
                nc.vector.tensor_tensor(rot[:, r], rot[:, r], swp[:, r], ALU.add).then_inc(rot_ready, 1)

            def ffn_x(u, j):
                dve.wait_ge(wo_done, u + 1)
                dve.wait_ge(y_ready, NT + u)
                nc.vector.tensor_tensor(xf[:, :].unsqueeze(1), bank[6][:, 0:P].unsqueeze(1),
                                        Y[:, bass.ds(u % NT, 1), :], ALU.add).then_inc(xf_ready, 1)

            def ffn_stats(u, j):
                dve.wait_ge(fback_done, u + 1)
                wait(dve, mv_ready, u)
                nc.vector.bn_stats(st[:, :], bank[6][:, 0:P]).then_inc(st_ready, 1)
                dve.wait_ge(st_ready, u + 1)
                wait(dve, rstd_ready, u)
                wait(dve, xn_ready, u)
                alone(dve)
                nc.vector.bn_aggr(mv[:, :], st[:, :]).then_inc(mv_ready, 1)

            def ffn_norm(u, j):
                dve.wait_ge(rstd_ready, u + 1)
                dve.wait_ge(mv_ready, u + 1)
                wait(dve, xnT_done, u)
                nc.vector.tensor_scalar(xn[:, :], bank[6][:, 0:P], mv[:, 0:1], rstd[:, 0:1],
                                        ALU.subtract, ALU.mult).then_inc(xn_ready, 1)

            def gated(u, j):
                dve.wait_ge(ge_ready, u + 1)
                dve.wait_ge(lin_done, u + 1)
                wait(dve, w2_done, u)
                for c, (h0, hn) in enumerate(HC):
                    last = nc.vector.scalar_tensor_tensor(
                        out=hh[0:hn, c, :], in0=bank[6][0:hn, c * P:(c + 1) * P], scalar=b1[0:hn, c:c + 1],
                        in1=ge[0:hn, c, :], op0=ALU.add, op1=ALU.mult)
                last.then_inc(hh_ready, 1)

            def ffn_y(u, j):
                dve.wait_ge(w2_done, u + 1)
                dve.wait_ge(xp_ready, u + 1)
                nc.vector.tensor_tensor(Y[:, bass.ds(u % NT, 1), :], bank[6][:, 0:P].unsqueeze(1),
                                        xf[:, :].unsqueeze(1), ALU.add).then_inc(y_ready, 1)

            def slot(g, gs):
                step(g, gs, 0, sumsq, 0)
                step(g, gs, 1, sums, 0)
                step(g, gs, 1, sums_inverse, 0)
                step(g, gs, 1, probs, 0)
                step(g, gs, 3, ffn_y)
                step(g, gs, 1, maxes, 1)
                step(g, gs, 1, less_max, 1)
                step(g, gs, 0, sumsq, 1)
                step(g, gs, 2, ffn_x)
                step(g, gs, 1, probs_before, 0)
                step(g, gs, 1, sums, 1)
                step(g, gs, 1, sums_inverse, 1)
                step(g, gs, 1, probs, 1)
                step(g, gs, 2, ffn_stats)
                step(g, gs, 0, normed, 0)
                step(g, gs, 1, probs_before, 1)
                step(g, gs, 2, ffn_norm)
                step(g, gs, 0, normed, 1)
                step(g, gs, 0, cos_part, 0)
                step(g, gs, 0, rotated, 0)
                step(g, gs, 0, cos_part, 1)
                step(g, gs, 0, rotated, 1)
                step(g, gs, 2, gated)
                step(g, gs, 0, maxes, 0)
                step(g, gs, 0, less_max, 0)

            slots(dve, slot)

            dve.wait_ge(y_ready, NT + NI)
            dve.wait_ge(a_x2, B)
            for b in range(B):
                yb = Y[:, b * TPB:(b + 1) * TPB, :]
                nc.vector.tensor_tensor(yb, yb, GB[:, b, :].unsqueeze(1).broadcast_to([P, TPB, D]), ALU.mult)\
                    .then_inc(fin_mul, 1)
                wait(dve, fin_mul, b + 1)
                nc.vector.tensor_tensor(yb, yb, X1[:, b * TPB:(b + 1) * TPB, :], ALU.add).then_inc(fin_ready, 1)


def kernel(**inputs):
    import concourse.bacc as bacc
    from concourse.bass_utils import run_bass_kernel_spmd

    f = lambda name: np.asarray(inputs[name])
    tc, ts, mask, eye = tables()
    col = lambda name: f(name).reshape(D, 1)
    arrays = {
        "x": f("L0_attn_x"),
        "wq": f("L0_attn_Wq").T, "wk": f("L0_attn_Wk").T, "wv": f("L0_attn_Wv").T, "wo": f("L0_attn_Wo").T,
        "bq": col("L0_attn_bq"), "bk": col("L0_attn_bk"), "bv": col("L0_attn_bv"), "bo": col("L0_attn_bo"),
        "cT": f("L0_c").T, "wmod": f("L0_wmod").reshape(D, 6, D),
        "wqkv": f("L0_ffn_Wqkv"), "qs": f("L0_ffn_q_scale"), "ks": f("L0_ffn_k_scale"), "fwo": f("L0_ffn_Wo"),
        "ln_g": f("L0_ffn_ln_g").reshape(DEPTH, D, 1), "ln_b": f("L0_ffn_ln_b").reshape(DEPTH, D, 1),
        "w1": f("L0_ffn_W1"), "b1": f("L0_ffn_b1").reshape(DEPTH, 2 * HID, 1),
        "w2": f("L0_ffn_W2"), "b2": f("L0_ffn_b2").reshape(DEPTH, 1, D),
        "tab_cos": tc, "tab_sin": ts, "mask": mask, "eye": eye,
    }
    arrays = {k: np.ascontiguousarray(v) for k, v in arrays.items()}
    nc = bacc.Bacc("TRN2", target_bir_lowering=False, num_devices=1)
    args = [nc.dram_tensor("d_" + k, v.shape, mybir.dt.from_np(v.dtype), kind="ExternalInput").ap()
            for k, v in arrays.items()]
    out = nc.dram_tensor("d_out", (B, S, D), F32, kind="ExternalOutput").ap()
    adaln_block(nc, *args, out)
    r = run_bass_kernel_spmd(nc, [{"d_" + k: v for k, v in arrays.items()}], core_ids=[0])
    return r.results[0]["d_out"]
```
